# Optimizing a Trainium2 kernel written in Bass

```python
import numpy as np
import jax
import jax.numpy as jnp

def _softmax(x, axis=-1):
    return jax.nn.softmax(x, axis=axis)

def _gelu(x):
    return jax.nn.gelu(x, approximate=True)

def _silu(x):
    return jax.nn.silu(x)

def _sigmoid(x):
    return jax.nn.sigmoid(x)

def _layernorm(x, axis=-1, eps=1e-05):
    m = jnp.mean(x, axis=axis, keepdims=True)
    v = jnp.var(x, axis=axis, keepdims=True)
    return (x - m) / jnp.sqrt(v + eps)

def _scatter_add(tgt, idx, src, axis=0):
    return tgt.at[idx].add(src)

def _segment_sum(src, seg, n):
    return jax.ops.segment_sum(src, seg, n)
kernel_name = 'mk_prb_d1_jaxref_r8_3481bb'

def setup_inputs(seed: int=0):
    np.random.seed(seed)
    _w = jnp.asarray

    def _L0_attn_setup():
        import jax, jax.numpy as jnp
        import numpy as np
        import math
        N_EMBED = 256
        N_HEAD = 16
        HEAD_DIM = N_EMBED // N_HEAD // 2
        LAYER = 2
        LAMBDA_INIT = 0.8 - 0.6 * math.exp(-0.3 * (LAYER - 1))
        B, T = (2, 256)
        EPS = 1e-05

        def _causal_sdpa(q, k, v):
            Tq = q.shape[2]
            scale = 1.0 / math.sqrt(q.shape[-1])
            scores = jnp.einsum('bhqd,bhkd->bhqk', q, k) * scale
            mask = jnp.tril(jnp.ones((Tq, Tq), dtype=bool))
            scores = jnp.where(mask, scores, -jnp.inf)
            probs = jax.nn.softmax(scores, axis=-1)
            return jnp.einsum('bhqk,bhkv->bhqv', probs, v)
        key = jax.random.key(seed)
        ks = jax.random.split(key, 7)
        s = 1.0 / math.sqrt(N_EMBED)
        return {'x': jax.random.normal(ks[0], (B, T, N_EMBED), dtype=jnp.float32), 'Wqkv': jax.random.normal(ks[1], (N_EMBED, 3 * N_EMBED), dtype=jnp.float32) * s, 'Wproj': jax.random.normal(ks[2], (N_EMBED, N_EMBED), dtype=jnp.float32) * s, 'lambda_q1': jax.random.normal(ks[3], (HEAD_DIM,), dtype=jnp.float32) * 0.1, 'lambda_k1': jax.random.normal(ks[4], (HEAD_DIM,), dtype=jnp.float32) * 0.1, 'lambda_q2': jax.random.normal(ks[5], (HEAD_DIM,), dtype=jnp.float32) * 0.1, 'lambda_k2': jax.random.normal(ks[6], (HEAD_DIM,), dtype=jnp.float32) * 0.1}
    _L0_attn_in = _L0_attn_setup()

    def _L0_ffn_setup():
        import jax, jax.numpy as jnp
        import numpy as np
        B, S, D = (4, 128, 256)
        H = 512
        NE = 8
        TOPK = 2
        key = jax.random.key(seed)
        ks = jax.random.split(key, 9)
        s = lambda fan_in: 1.0 / np.sqrt(fan_in)
        return {'x': jax.random.normal(ks[0], (B, S, D), dtype=jnp.float32), 'W1': jax.random.normal(ks[1], (NE, D, H), dtype=jnp.float32) * s(D), 'b1': jnp.zeros((NE, H), dtype=jnp.float32), 'W2': jax.random.normal(ks[2], (NE, H, H), dtype=jnp.float32) * s(H), 'b2': jnp.zeros((NE, H), dtype=jnp.float32), 'W3': jax.random.normal(ks[3], (NE, H, D), dtype=jnp.float32) * s(H), 'b3': jnp.zeros((NE, D), dtype=jnp.float32), 'Wg': jax.random.normal(ks[4], (D, NE), dtype=jnp.float32) * s(D), 'bg': jnp.zeros((NE,), dtype=jnp.float32)}
    _L0_ffn_in = _L0_ffn_setup()
    _d = {'L0_attn_x': _L0_attn_in['x'], 'L0_attn_Wqkv': _L0_attn_in['Wqkv'], 'L0_attn_Wproj': _L0_attn_in['Wproj'], 'L0_attn_lambda_q1': _L0_attn_in['lambda_q1'], 'L0_attn_lambda_k1': _L0_attn_in['lambda_k1'], 'L0_attn_lambda_q2': _L0_attn_in['lambda_q2'], 'L0_attn_lambda_k2': _L0_attn_in['lambda_k2'], 'L0_ffn_W1': _L0_ffn_in['W1'], 'L0_ffn_b1': _L0_ffn_in['b1'], 'L0_ffn_W2': _L0_ffn_in['W2'], 'L0_ffn_b2': _L0_ffn_in['b2'], 'L0_ffn_W3': _L0_ffn_in['W3'], 'L0_ffn_b3': _L0_ffn_in['b3'], 'L0_ffn_Wg': _L0_ffn_in['Wg'], 'L0_ffn_bg': _L0_ffn_in['bg']}
    _x0 = _d['L0_attn_x']
    _d['L0_attn_x'] = jax.random.normal(jax.random.fold_in(jax.random.key(seed), 1), (4, 512, 256), dtype=_x0.dtype)
    del _x0
    return _d

def reference(L0_attn_x, L0_attn_Wqkv, L0_attn_Wproj, L0_attn_lambda_q1, L0_attn_lambda_k1, L0_attn_lambda_q2, L0_attn_lambda_k2, L0_ffn_W1, L0_ffn_b1, L0_ffn_W2, L0_ffn_b2, L0_ffn_W3, L0_ffn_b3, L0_ffn_Wg, L0_ffn_bg):

    def _L0_attn_ref(x, Wqkv, Wproj, lambda_q1, lambda_k1, lambda_q2, lambda_k2):
        import jax, jax.numpy as jnp
        import numpy as np
        import math
        N_EMBED = 256
        N_HEAD = 16
        HEAD_DIM = N_EMBED // N_HEAD // 2
        LAYER = 2
        LAMBDA_INIT = 0.8 - 0.6 * math.exp(-0.3 * (LAYER - 1))
        B, T = (2, 256)
        EPS = 1e-05

        def _causal_sdpa(q, k, v):
            Tq = q.shape[2]
            scale = 1.0 / math.sqrt(q.shape[-1])
            scores = jnp.einsum('bhqd,bhkd->bhqk', q, k) * scale
            mask = jnp.tril(jnp.ones((Tq, Tq), dtype=bool))
            scores = jnp.where(mask, scores, -jnp.inf)
            probs = jax.nn.softmax(scores, axis=-1)
            return jnp.einsum('bhqk,bhkv->bhqv', probs, v)
        Bx, Tx, Cfull = x.shape
        C = Cfull // 2
        qkv = x @ Wqkv
        q1, k1, q2, k2, v = jnp.split(qkv, [C, 2 * C, 3 * C, 4 * C], axis=-1)

        def heads(t, d):
            return t.reshape(Bx, Tx, N_HEAD, d).transpose(0, 2, 1, 3)
        q1, k1, q2, k2 = (heads(t, HEAD_DIM) for t in (q1, k1, q2, k2))
        v = heads(v, 2 * HEAD_DIM)
        lam = jnp.exp(jnp.dot(lambda_q1, lambda_k1)) - jnp.exp(jnp.dot(lambda_q2, lambda_k2)) + LAMBDA_INIT
        A1 = _causal_sdpa(q1, k1, v)
        A2 = _causal_sdpa(q2, k2, v)
        diff = A1 - lam * A2
        rms = jnp.sqrt(jnp.mean(diff * diff, axis=-1, keepdims=True) + EPS)
        diff = diff / rms
        diff = (1.0 - LAMBDA_INIT) * diff
        out = diff.transpose(0, 2, 1, 3).reshape(Bx, Tx, Cfull)
        return out @ Wproj

    def _L0_ffn_ref(x, W1, b1, W2, b2, W3, b3, Wg, bg):
        import jax, jax.numpy as jnp
        import numpy as np
        B, S, D = (4, 128, 256)
        H = 512
        NE = 8
        TOPK = 2
        gate_logits = jnp.einsum('bsd,dn->bsn', x, Wg) + bg
        gate_weights = jax.nn.softmax(gate_logits, axis=-1)
        topv, topi = jax.lax.top_k(gate_weights, TOPK)
        h = jax.nn.gelu(jnp.einsum('bsd,ndh->nbsh', x, W1) + b1[:, None, None, :], approximate=False)
        h = jax.nn.gelu(jnp.einsum('nbsh,nhf->nbsf', h, W2) + b2[:, None, None, :], approximate=False)
        eo = jnp.einsum('nbsf,nfd->nbsd', h, W3) + b3[:, None, None, :]
        comb = jnp.sum(jax.nn.one_hot(topi, NE, dtype=x.dtype) * topv[..., None], axis=-2)
        out = jnp.einsum('nbsd,bsn->bsd', eo, comb)
        return out
    x = L0_attn_x
    xn = _layernorm(x, axis=-1)
    x = x + _L0_attn_ref(xn, L0_attn_Wqkv, L0_attn_Wproj, L0_attn_lambda_q1, L0_attn_lambda_k1, L0_attn_lambda_q2, L0_attn_lambda_k2) + _L0_ffn_ref(xn, L0_ffn_W1, L0_ffn_b1, L0_ffn_W2, L0_ffn_b2, L0_ffn_W3, L0_ffn_b3, L0_ffn_Wg, L0_ffn_bg)
    return x

_drawn_inputs = setup_inputs


def setup_inputs(seed=0):
    import zlib

    import numpy as np

    out = dict(_drawn_inputs(seed))
    spreads = {'L0_ffn_b1': (0.0, 0.525),
     'L0_ffn_b2': (0.0, 0.354),
     'L0_ffn_b3': (0.0, 0.1),
     'L0_ffn_bg': (0.0, 0.287)}
    factors = {'L0_attn_lambda_k1': 8.0, 'L0_attn_lambda_q2': 5.879, 'L0_attn_lambda_k2': 3.426}
    for name, (base, spread) in spreads.items():
        noise = np.random.default_rng([zlib.crc32(name.encode()), seed]).standard_normal(out[name].shape)
        drawn = base * np.exp(spread * noise) if base else spread * noise
        out[name] = jnp.asarray(drawn.astype(out[name].dtype))
    for name, factor in factors.items():
        out[name] = (out[name] * factor).astype(out[name].dtype)
    return out
```

```python
import math
from contextlib import ExitStack

import numpy as np

import concourse.bass as bass
from concourse import mybir

ALU = mybir.AluOpType
ACT = mybir.ActivationFunctionType
F32 = mybir.dt.float32
BF16 = mybir.dt.bfloat16
I32 = mybir.dt.int32
X = mybir.AxisListType.X

P = 128
EPS = 1e-5
NEG = -1e30


class Steps:

    def __init__(self, eng, sem):
        self.eng, self.sem, self.n, self.before = eng, sem, 0, 0

    def done(self, ins):
        ins.then_inc(self.sem, 1)
        self.n += 1

    def wait(self):
        self.eng.wait_ge(self.sem, self.before + self.n)

    def then_wait(self, ins):
        self.done(ins)
        self.wait()


def build(nc, x, Wqkv, Wproj, lq1, lk1, lq2, lk2, W1, b1, W2, b2, W3, b3, Wg, bg, out):
    B, T, D = x.shape
    NE, _, H = W1.shape
    N = B * T
    TT = N // P
    KB = T // P
    NH, HD, VD = 16, 8, 16
    KC = D // P
    HC = H // P
    HG = NH // 4
    GROUPS = 6
    STACK = GROUPS * HD
    MAX_AT = P - 3
    NT = (2 * N) // P + NE - 1
    UNITS = B * HG * 2
    LAMBDA_INIT = 0.8 - 0.6 * math.exp(-0.3)
    SCALE = 1.0 / math.sqrt(HD)
    VW = VD + 1
    Q_IN = (slice(0, 3), slice(3, 5), slice(5, 6))
    K_IN = (slice(1, 6, 2), slice(0, 5, 4), slice(2, 3))

    def scratch(name, shape, dtype):
        return nc.dram_tensor(name, shape, dtype).ap()

    q_stack = scratch("q_stack", [2, B * NH, HD, GROUPS, T], BF16)
    k_stack = scratch("k_stack", [2, B * NH, HD, GROUPS, T], BF16)
    xn_rows = scratch("xn_rows", [N + P, D], F32)
    slot_rows = scratch("slot_rows", [P * (NT + 1), 2], F32)
    sums = scratch("sums", [N + P, D], F32)
    bias_rows = scratch("bias_rows", [3, NE, 2 * H + D], BF16)

    with ExitStack() as ctx:
        def sb(name, shape, dt):
            return ctx.enter_context(nc.sbuf_tensor(name, shape, dt))

        def sem(name):
            return ctx.enter_context(nc.semaphore(name))

        bank = [ctx.enter_context(nc.psum_tensor(f"bank{k}", [P, 512], F32)) for k in range(8)]

        W12 = NE * (KC + HC) * H
        big = sb("big", [P, W12], F32)
        w1_sb = big[:, 0:NE * KC * H]
        w2_sb = big[:, NE * KC * H:W12]
        q_words = 4 * 4 * T // 2
        late_experts = q_words // (KC * H)
        assert late_experts * KC * H == q_words
        q_at = (NE - late_experts) * KC * H
        q_ring = big[:, q_at:q_at + q_words].bitcast(BF16).rearrange("p (r h n) -> p r h n", r=4, h=4)
        taken = [0]

        def in_big(n, dtype=F32):
            words = n if dtype in (F32, I32) else n // 2
            v = big[:, taken[0]:taken[0] + words]
            taken[0] += words
            return v if dtype == F32 else v.bitcast(dtype)

        xn_all = in_big(TT * D).rearrange("p (t d) -> p t d", t=TT)
        assert taken[0] <= q_at
        taken[0] = q_at + q_words
        xnT = in_big(2 * KC * T).rearrange("p (r k n) -> p r k n", r=2, k=KC)
        wqk = in_big(KC * 2 * D).rearrange("p (k n) -> p k n", k=KC)
        wvg = in_big(KC * (D + NE)).rearrange("p (k n) -> p k n", k=KC)
        rest = in_big(2 * T).rearrange("p (r n) -> p r n", r=2)
        parts = in_big(2 * 3 * T, BF16).rearrange("p (r c n) -> p r c n", r=2, c=3)
        stats = in_big(TT * 6).rearrange("p (t s) -> p t s", s=6)
        mv = in_big(TT * 2).rearrange("p (t s) -> p t s", s=2)
        ve = in_big(TT)
        sd = in_big(TT)
        rstd = in_big(TT)
        nwt = in_big(TT)
        route = [in_big(TT * NE).rearrange("p (t e) -> p t e", e=NE) for _ in range(6)]
        logits, eq, oh1, oh2, lg2, pos = route
        ex9 = in_big(TT * 9).rearrange("p (t e) -> p t e", e=9)
        oh12 = in_big(TT * NE, BF16).rearrange("p (t e) -> p t e", e=NE)
        small = [in_big(TT) for _ in range(6)]
        m1, wm, m2, wm2, esum, w2u = small
        rev8 = in_big(NE)
        thr = in_big(TT)
        bgb = in_big(NE)
        cnt = in_big(NE)
        full = in_big(NE * TT).rearrange("p (e j) -> p e j", e=NE)
        ctile = in_big(NE)
        base = in_big(NE)
        base128 = in_big(NE)
        tile_no = in_big(NT + 1)
        past = in_big((NT + 1) * (NE - 1)).rearrange("p (j e) -> p j e", j=NT + 1)
        texp_f = in_big(NT + 1)
        slot_f = in_big(2 * TT)
        slot_lo = in_big(2 * TT, I32)
        slot_hi = in_big(2 * TT, I32)
        slots_i = in_big(2 * TT, I32)
        no_slot = in_big(2 * (NT + 1)).rearrange("p (j c) -> p j c", c=2)
        lam_in = in_big(4 * HD).rearrange("p (a d) -> p a d", a=4)
        lam_pr = in_big(2 * HD).rearrange("p (a d) -> p a d", a=2)
        lam_d = in_big(2)
        lam_e = in_big(2)
        bias_in = in_big(2 * H + D)
        bias_r = in_big(2 * H + D)
        bias_p = in_big(3 * (2 * H + D), BF16).rearrange("p (c n) -> p c n", c=3)
        minus1 = in_big(2 * T, BF16)
        assert taken[0] <= W12

        x_all = sb("x_all", [P, TT, D], F32)
        d_all = sb("d_all", [P, 1 + B * HG // 2, KB, 2, 4 * VD], F32)
        slot_at = sb("slot_at", [P, 2 * TT], I32)
        pairs = sb("pairs", [P, 2 * TT, 2], F32)
        wts = pairs[:, :, 1].rearrange("p (c t) -> p c t", c=2)
        at_now = sb("at_now", [P, 4, 1], I32)
        pair_now = sb("pair_now", [P, 4, 2], F32)
        texp = sb("texp", [P, NT + 1], I32)
        slot_sb = sb("slot_sb", [P, NT + 1, 2], F32)
        neglam = sb("neglam", [P, 1], F32)
        wproj_sb = sb("wproj_sb", [P, KC, D], F32)
        ident = sb("ident", [P, P], F32)
        identb = sb("identb", [P, P], BF16)
        causal = sb("causal", [P, P], BF16)
        below = sb("below", [P, P], BF16)
        onesb = sb("onesb", [P, P], BF16)

        half = 4 * 2 * T // 2
        pt_at = [4 * sum(T - P * j for j in range(kb)) for kb in range(KB + 1)]
        shared = sb("shared", [P, max(NE * HC * D, half + pt_at[KB])], F32)
        w3_sb = shared[:, 0:NE * HC * D]
        k_ring = shared[:, 0:half].bitcast(BF16).rearrange("p (r j n) -> p r j n", r=4, j=2)
        pt = [shared[:, half + pt_at[kb]:half + pt_at[kb + 1]].rearrange("p (h n) -> p h n", h=4)
              for kb in range(KB)]
        v_words = B * HG * KB * 4 * VW
        vbuf = sb("vbuf", [P, v_words + 2 * KB * 4 * 32], F32)
        v_all = vbuf[:, 0:v_words].rearrange("p (g k h e) -> p g k h e", g=B * HG, k=KB, h=4)
        v_unit = vbuf[:, v_words:v_words + 2 * KB * 4 * 32].rearrange(
            "p (r k h e) -> p r k h e", r=2, k=KB, h=4)
        bias_sb = vbuf[0:3, 0:NE * (2 * H + D) // 2].bitcast(BF16)
        assert NE * (2 * H + D) // 2 <= v_words + 2 * KB * 4 * 32
        mx = sb("mx", [P, 2, 4, KB], F32)
        mrest = sb("mrest", [P, 2, 4, KB], F32)
        mparts = sb("mparts", [P, 2, KB, 4, 3], BF16)
        mT = sb("mT", [12, 2, T], BF16)
        outT = sb("outT", [P, 2, T], F32)
        dT_b = sb("dT_b", [P, KC, T], F32)
        rsum = sb("rsum", [P, 2, 4 * KB], F32)
        a1 = sb("a1", [P, 4 * KB, VD], F32)
        a2 = sb("a2", [P, 4 * KB, VD], F32)
        squares = sb("squares", [P, KB, 4 * VD], F32)
        ssq = sb("ssq", [P, 1 + B * HG // 2, KB, 2, 4], F32)
        ssq_b = ssq[:, 1:].rearrange("p (b g) t s h -> p b (g t s h)", b=B)
        rms = sb("rms", [P, B, HG * KB * 4], F32)
        rinv = sb("rinv", [P, B, HG * KB * 4], F32)
        xg = sb("xg", [P, 2, D], F32)
        late = d_all[:, :, :, :, :].rearrange("p g t s n -> p (g t s n)")
        hbuf = late[:, 0:2 * H].rearrange("p (q n) -> p q n", q=2)
        hT = late[:, 2 * H:4 * H].rearrange("p (q k n) -> p q k n", q=2, k=HC)
        xT = late[:, 4 * H:4 * H + 2 * D].rearrange("p (q k n) -> p q k n", q=2, k=KC)
        ybuf = late[:, 4 * H + 2 * D:4 * H + 4 * D].rearrange("p (q n) -> p q n", q=2)
        token_i = sb("token_i", [P, NT + 1], I32)
        idx = sb("idx", [P, 3, 1], I32)

        x_in = [sem(f"x_in{b}") for b in range(B)]
        w_in = sem("w_in")
        consts = sem("consts")
        ln = sem("ln")
        ve_ready = sem("ve_ready")
        sd_ready = sem("sd_ready")
        xn_ready = sem("xn_ready")
        xnT_ps = sem("xnT_ps")
        xnT_ready = sem("xnT_ready")
        qk_ps = sem("qk_ps")
        part0 = sem("part0")
        rest_ready = sem("rest_ready")
        part1 = sem("part1")
        part2 = sem("part2")
        stacked = [sem("stacked0"), sem("stacked1")]
        vg_ps = sem("vg_ps")
        v_copied = sem("v_copied")
        lg_ready = sem("lg_ready")
        rt = sem("rt")
        ex9_in = sem("ex9_in")
        ex9_out = sem("ex9_out")
        oh_ready = sem("oh_ready")
        rank_ps = sem("rank_ps")
        slots_ready = sem("slots_ready")
        lam_ready = sem("lam_ready")
        lam_exp = sem("lam_exp")
        bias_step = sem("bias_step")
        bias_parts = sem("bias_parts")
        bias_saved = sem("bias_saved")
        xn_saved = sem("xn_saved")
        slot_zero = sem("slot_zero")
        scattered = [sem(f"scattered{k}") for k in range(4)]
        w12_in = sem("w12_in")
        rings_set = sem("rings_set")
        minus_in = sem("minus_in")
        unit_in = [sem(f"unit_in{r}") for r in range(4)]
        max_rows = [sem(f"max_rows{r}") for r in range(4)]
        s_ps = sem("s_ps")
        s_read = sem("s_read")
        mx_step = sem("mx_step")
        mp_ready = sem("mp_ready")
        mT_ps = sem("mT_ps")
        mT_ready = sem("mT_ready")
        st_ps = sem("st_ps")
        exp_done = sem("exp_done")
        masked = sem("masked")
        v_ready = sem("v_ready")
        pv_done = sem("pv_done")
        outT_ready = sem("outT_ready")
        o_ps = sem("o_ps")
        o_read = sem("o_read")
        at_step = sem("at_step")
        ep = sem("ep")
        ssq_ready = sem("ssq_ready")
        rms_ready = sem("rms_ready")
        dn_ready = [sem("dn_ready0"), sem("dn_ready1")]
        dT_ps = sem("dT_ps")
        dT_ready = sem("dT_ready")
        proj_ps = sem("proj_ps")
        proj_read = sem("proj_read")
        w3_in = sem("w3_in")
        bias_in_sb = sem("bias_in_sb")
        idx_ready = sem("idx_ready")
        gathered = [sem("gathered0"), sem("gathered1")]
        xT_ps = sem("xT_ps")
        xT_ready = sem("xT_ready")
        l_ps = [sem("l1_ps"), sem("l2_ps")]
        h_ready = [sem("h1_ready"), sem("h2_ready")]
        hT_ps = [sem("h1T_ps"), sem("h2T_ps")]
        hT_ready = [sem("h1T_ready"), sem("h2T_ready")]
        y_ps = sem("y_ps")
        y_ready = sem("y_ready")
        added = sem("added")
        rows_free = sem("rows_free")
        sums_in = sem("sums_in")
        pool_on = sem("pool_on")
        pool_step = sem("pool_step")
        diff_done = sem("diff_done")
        ssq_done = sem("ssq_done")
        norms_ready = sem("norms_ready")
        slots_in = sem("slots_in")
        out_saved = sem("out_saved")

        dT = (outT, dT_b)
        xv = x.rearrange("b (k p) d -> b p k d", p=P)
        outv = out.rearrange("b (k p) d -> b p k d", p=P)

        def groups_of(width):
            gs = []
            for t in range(KB):
                heads = 2 if 2 * width(t) <= 512 else 1
                gs += [(t, h, heads, width(t)) for h in range(0, 4, heads)]
            return gs

        A_GROUPS = groups_of(lambda t: P * (t + 1))
        B_GROUPS = groups_of(lambda t: T - P * t)
        NG = len(A_GROUPS)
        A_BANKS, B_BANKS = (bank[0], bank[1], bank[7]), (bank[2], bank[3])
        assert NG % 3 == 0 and NG % 2 == 0 and len(B_GROUPS) == NG
        B_LAST = [max(n for n, g in enumerate(B_GROUPS) if g[0] == kb) for kb in range(KB)]

        def unit_loop(eng, body):
            with eng.Fori(0, UNITS // 4 - 1) as i:
                for r in range(4):
                    body(i, r, False)
            for r in range(4):
                body(UNITS // 4 - 1, r, True)

        assert NT % 2 == 1

        def tile_loop(eng, body):
            with eng.Fori(0, NT // 2) as i:
                body(i, (0, 1), False)
            body(NT // 2, (0,), True)

        def scale_pair(eng, b, k):
            d = d_all[:, 1 + b * HG // 2 + k].rearrange("p t s (h e) -> p (t s h) e", e=VD)
            return eng.tensor_tensor(d, d, rinv[:, b, k * 8 * KB:(k + 1) * 8 * KB].unsqueeze(2).to_broadcast(
                [P, 8 * KB, VD]), ALU.mult)

        def row(v, j):
            if isinstance(j, int):
                return v[j]
            names = "abcd"[:len(v.shape) - 2]
            return v[bass.ds(j, 1)].rearrange(f"o y {' '.join(names)} -> (o y) {' '.join(names)}")

        def column(v, j):
            if isinstance(j, int):
                return v[:, j]
            names = "abcd"[:len(v.shape) - 3]
            return v[:, bass.ds(j, 1)].rearrange(f"p o y {' '.join(names)} -> p (o y) {' '.join(names)}")

        W_IN = 16 * (3 + 1 + 4 + 3 + 1)
        CONSTS = 17
        RT_STEPS = 43

        block = ctx.enter_context(nc.Block())

        w1v = w1_sb.rearrange("p (e k n) -> p e k n", e=NE, k=KC)
        w2v = w2_sb.rearrange("p (e k n) -> p e k n", e=NE, k=HC)

        @block.sync
        def _(sp):
            for b in range(B):
                sp.dma_start(x_all[:, b * KB:(b + 1) * KB, :], xv[b]).then_inc(x_in[b], 16)
                if b == 0:
                    wq = Wqkv.rearrange("(k p) n -> p k n", p=P)
                    sp.dma_start(wqk, wq[:, :, 0:2 * D]).then_inc(w_in, 16)
                    sp.dma_start(wvg[:, :, 0:D], wq[:, :, 2 * D:3 * D]).then_inc(w_in, 16)
                    sp.dma_start(wvg[:, :, D:D + NE], Wg.rearrange("(k p) n -> p k n", p=P)
                                 ).then_inc(w_in, 16)
            def load(i, r):
                if not (isinstance(i, int) and 4 * i + r < 3):
                    sp.wait_ge(exp_done, NG * (4 * i + r - 3) + 2)
                def heads(stack, s):
                    return row(stack[r % 2].rearrange("(g s j) d c n -> s g (d c) j n", s=2, j=2)[s],
                               2 * i + r // 2)

                for s in range(2):
                    rows = slice(STACK * s, STACK * (s + 1))
                    sp.dma_start(q_ring[rows, r, 2 * s:2 * s + 2, :], heads(q_stack, s)
                                 ).then_inc(unit_in[r], 16)
                    sp.dma_start(k_ring[rows, r, :, :], heads(k_stack, s)).then_inc(unit_in[r], 16)

            def put_max(i, r):
                sp.wait_ge(mT_ready, 4 * i + r + 1)
                for hh in range(4):
                    sp.dma_start(q_ring[MAX_AT:P, r, hh, :], mT[3 * hh:3 * hh + 3, r % 2, :]
                                 ).then_inc(max_rows[r], 16)

            n = 0
            for b in range(B):
                for f in range(4):
                    stack = (q_stack, k_stack)[f % 2][f // 2][b * NH:(b + 1) * NH]
                    stack = stack.rearrange("h d g n -> (h d) g n")
                    for c, ready in enumerate((part0, part1, part2)):
                        sp.wait_ge(ready, n + 1)
                        to = stack[:, (Q_IN, K_IN)[f % 2][c]]
                        sp.dma_start(to, parts[:, n % 2, c, :].unsqueeze(1).to_broadcast(list(to.shape))
                                     ).then_inc(stacked[n % 2], 16)
                    n += 1
                if b == 1:
                    sp.wait_ge(stacked[0], 16 * 3 * 4)
                    sp.wait_ge(stacked[1], 16 * 3 * 4)
                    sp.wait_ge(minus_in, 16 * 4)
                    sp.wait_ge(rings_set, 2)
                    for u in range(3):
                        load(0, u)
            sp.wait_ge(xn_ready, TT)
            sp.dma_start(xn_rows[N:], xn_all[:, 0, :]).then_inc(xn_saved, 16)
            sp.dma_start(xn_rows[0:N].rearrange("(t p) d -> p t d", p=P), xn_all).then_inc(xn_saved, 16)
            sp.wait_ge(stacked[0], 16 * 3 * 8)
            sp.wait_ge(stacked[1], 16 * 3 * 8)
            put_max(0, 0)
            sp.wait_ge(bias_parts, 1)
            sp.dma_start(bias_rows.rearrange("c e n -> e c n"), bias_p[0:NE]).then_inc(bias_saved, 16)

            def step(i, r, tail):
                if not (tail and r == 3):
                    put_max(i + (r + 1) // 4, (r + 1) % 4)
                if not (tail and r > 0):
                    load(i + (r + 3) // 4, (r + 3) % 4)

            unit_loop(sp, step)

            sp.wait_ge(exp_done, NG * UNITS + 2)
            sp.wait_ge(pv_done, KB * UNITS + KB)
            w3v = w3_sb.rearrange("p (e k n) -> p e k n", e=NE, k=HC)
            for e in range(NE):
                sp.dma_start(w3v[:, e, :, :], W3[e].rearrange("(k p) n -> p k n", p=P)
                             ).then_inc(w3_in, 16)
                if e >= NE - late_experts:
                    sp.dma_start(w1v[:, e], W1[e].rearrange("(k p) n -> p k n", p=P)).then_inc(w3_in, 16)
            sp.wait_ge(bias_saved, 16)
            sp.dma_start(bias_sb, bias_rows.rearrange("c e n -> c (e n)")).then_inc(bias_in_sb, 16)

            for b in range(B):
                sp.wait_ge(proj_read, KB * (b + 1))
                sp.dma_start(sums[b * T:(b + 1) * T].rearrange("(k p) d -> p k d", p=P),
                             x_all[:, b * KB:(b + 1) * KB, :]).then_inc(sums_in, 16)
            sp.dma_start(sums[N:], x_all[:, 0, :]).then_inc(sums_in, 16)
            sp.wait_ge(added, 16 * NT)
            sp.dma_start(out.rearrange("b (p t) d -> (b p) (t d)", p=P // B),
                         sums[0:N].rearrange("(p t) d -> p (t d)", p=P)).then_inc(out_saved, 16)
            sp.wait_ge(out_saved, 16)

        @block.gpsimd
        def _(pool):
            own = Steps(pool, consts)
            own.done(pool.memset(ident[:, :], 0.0))
            own.done(pool.memset(identb[:, :], 0.0))
            own.done(pool.memset(causal[:, :], 0.0))
            own.done(pool.memset(below[:, :], 1.0))
            own.done(pool.memset(onesb[:, :], 1.0))
            own.done(pool.memset(minus1[0:3, :], -1.0))
            own.done(pool.memset(no_slot[:, :, 1], 0.0))
            own.wait()
            for m in (ident, identb):
                own.done(pool.affine_select(out=m[:, :], in_=m[:, :], compare_op=ALU.not_equal, fill=1.0,
                                            base=0, pattern=[[-1, P]], channel_multiplier=1))
            own.done(pool.affine_select(out=causal[:, :], in_=causal[:, :], compare_op=ALU.is_ge, fill=NEG,
                                        base=0, pattern=[[-1, P]], channel_multiplier=1))
            own.done(pool.affine_select(out=below[:, :], in_=below[:, :], compare_op=ALU.is_gt, fill=0.0,
                                        base=0, pattern=[[1, P]], channel_multiplier=-1))
            own.done(pool.iota(rev8, pattern=[[-1, NE]], base=NE, channel_multiplier=0,
                               allow_small_or_imprecise_dtypes=True))
            own.done(pool.iota(thr, pattern=[[P, TT]], base=0, channel_multiplier=0,
                               allow_small_or_imprecise_dtypes=True))
            own.done(pool.iota(tile_no, pattern=[[1, NT + 1]], base=0, channel_multiplier=0,
                               allow_small_or_imprecise_dtypes=True))
            for c in range(2):
                own.done(pool.iota(pairs[:, c * TT:(c + 1) * TT, 0], pattern=[[P, TT]], base=0,
                                   channel_multiplier=1, allow_small_or_imprecise_dtypes=True))
            own.done(pool.iota(no_slot[:, :, 0], pattern=[[0, NT + 1]], base=N, channel_multiplier=1,
                               allow_small_or_imprecise_dtypes=True))
            assert own.n == CONSTS
            pool.memset(q_ring[:, :, :, :], 0.0).then_inc(rings_set, 1)
            pool.memset(k_ring[:, :, :, :], 0.0).then_inc(rings_set, 1)
            pool.memset(vbuf[:, v_words:], 0.0).then_inc(rings_set, 1)
            pool.memset(v_all[:, :, :, :, VD:VW], 1.0).then_inc(rings_set, 1)
            pool.wait_ge(consts, CONSTS)
            pool.wait_ge(rings_set, 2)
            for r in range(4):
                pool.dma_start(k_ring[MAX_AT:P, r, :, :], minus1[0:3, :].rearrange("p (j n) -> p j n", j=2)
                               ).then_inc(minus_in, 16)
            pool.dma_start(slot_rows.rearrange("(p j) c -> p j c", p=P), no_slot).then_inc(slot_zero, 16)
            pool.wait_ge(w_in, W_IN)

            bs = Steps(pool, bias_step)
            nb = slice(0, NE)
            n = 0
            for b in range(B):
                for f in range(4):
                    pool.wait_ge(part1, n + 1)
                    pool.tensor_tensor(parts[:, n % 2, 2, :], rest[:, n % 2, :], parts[:, n % 2, 1, :],
                                       ALU.subtract).then_inc(part2, 1)
                    n += 1
                if b == 0:
                    bs.then_wait(pool.tensor_copy(bias_p[nb, 0, :], bias_in[nb, :]))
                if b == 1:
                    bs.then_wait(pool.tensor_tensor(bias_r[nb, :], bias_in[nb, :], bias_p[nb, 0, :],
                                                    ALU.subtract))
                if b == 2:
                    bs.then_wait(pool.tensor_copy(bias_p[nb, 1, :], bias_r[nb, :]))
            pool.tensor_tensor(bias_p[nb, 2, :], bias_r[nb, :], bias_p[nb, 1, :], ALU.subtract
                               ).then_inc(bias_parts, 1)

            pool.wait_ge(v_copied, TT)
            pool.wait_ge(rings_set, 4)
            pool.tensor_copy(v_unit[:, 0, :, :, 0:VW], v_all[:, 0]).then_inc(v_ready, 1)
            pool.wait_ge(slots_ready, 1)
            pool.wait_ge(slot_zero, 16)
            pool.wait_ge(rt, RT_STEPS)
            pr = Steps(pool, pool_step)

            def scatter_slots(i, r):
                pr.done(pool.tensor_copy(at_now[:, r, :], column(slot_at[:, :].unsqueeze(2), 4 * i + r)))
                pr.done(pool.tensor_copy(pair_now[:, r, :], column(pairs, 4 * i + r)))
                pr.wait()
                pool.sem_inc(pool_on, 1)
                pool.indirect_dma_start(out=slot_rows, out_offset=bass.IndirectOffsetOnAxis(
                    ap=at_now[:, r, :], axis=0), in_=pair_now[:, r, :], in_offset=None
                ).then_inc(scattered[r], 16)

            def difference(i, r):
                d = column(d_all, i + r // 2)[:, :, 1 - r // 2, :]
                pool.wait_ge(o_read, 4 * i + r + 1 + 1)
                pool.sem_inc(pool_on, 1)
                pool.tensor_tensor(d, a1[:, :, :].rearrange("p (t h) e -> p t (h e)", h=4),
                                   a2[:, :, :].rearrange("p (t h) e -> p t (h e)", h=4), ALU.add
                                   ).then_inc(diff_done, 1)
                pool.wait_ge(diff_done, 2 * i + r // 2 + 1)
                pool.sem_inc(pool_on, 1)
                pr.then_wait(pool.tensor_tensor(squares[:, :, :], d, d, ALU.mult))
                sq = squares[:, :, :].rearrange("p t (h e) -> p t h e", h=4)
                for n in (8, 4, 2):
                    pr.then_wait(pool.tensor_tensor(sq[:, :, :, 0:n], sq[:, :, :, 0:n], sq[:, :, :, n:2 * n],
                                                    ALU.add))
                pool.sem_inc(pool_on, 1)
                pool.tensor_tensor(column(ssq, i + r // 2)[:, :, 1 - r // 2, :].unsqueeze(3), sq[:, :, :, 0:1],
                                   sq[:, :, :, 1:2], ALU.add).then_inc(ssq_done, 1)

            STEPS_OF_4 = 4 * 2 + 2 * 4

            def step(i, r, tail):
                if r == 0:
                    pr.before, pr.n = STEPS_OF_4 * i, 0
                scatter_slots(i, r)
                if r % 2 == 1 and not (tail and r == 3):
                    pool.wait_ge(pv_done, KB * (4 * i + r))
                    g = 2 * i + (r + 1) // 2
                    pool.tensor_copy(v_unit[:, (r + 1) // 2 % 2, :, :, 0:VW], column(v_all, g)
                                     ).then_inc(v_ready, 1)
                for kb in range(KB):
                    pool.wait_ge(exp_done, NG * (4 * i + r) + B_LAST[kb] + 1 + 2)
                    pool.sem_inc(pool_on, 1)
                    diag = pt[kb][:, :, 0:P]
                    pool.affine_select(out=diag, in_=diag, compare_op=ALU.is_ge, fill=0.0, base=0,
                                       pattern=[[0, 4], [1, P]], channel_multiplier=-1).then_inc(masked, 1)
                if r % 2 == 0:
                    difference(i, r)
                pool.wait_ge(scattered[r], 16 * (i + 1))
                assert r < 3 or pr.n == STEPS_OF_4

            unit_loop(pool, step)

            difference(UNITS // 4, 0)

            for b in range(B):
                pool.wait_ge(norms_ready, b + 1)
                scale_pair(pool, b, 1).then_inc(dn_ready[1], 1)

            pool.dma_start(slot_sb[:, :, :], slot_rows.rearrange("(p j) c -> p j c", p=P)).then_inc(slots_in, 16)
            pool.wait_ge(slots_in, 16)

            ix = Steps(pool, idx_ready)
            ix.done(pool.tensor_copy(token_i[:, :], slot_sb[:, :, 0]))

            def gather(i, q):
                pool.wait_ge(xT_ps, 2 * i + q + 1)
                ix.done(pool.tensor_copy(idx[:, q, :], column(token_i[:, :].unsqueeze(2), 2 * i + q)))
                ix.wait()
                pool.sem_inc(pool_on, 1)
                pool.indirect_dma_start(out=xg[:, q, :], out_offset=None, in_=xn_rows,
                                        in_offset=bass.IndirectOffsetOnAxis(ap=idx[:, q, :], axis=0)
                                        ).then_inc(gathered[q], 16)

            def add_rows(i, q):
                ix.done(pool.tensor_copy(idx[:, 2, :], column(token_i[:, :].unsqueeze(2), 2 * i + q)))
                ix.wait()
                pool.wait_ge(y_ready, 2 * i + q + 1 + 2)
                pool.sem_inc(pool_on, 1)
                pool.indirect_dma_start(out=sums, out_offset=bass.IndirectOffsetOnAxis(
                    ap=idx[:, 2, :], axis=0), in_=ybuf[:, q, :], in_offset=None,
                    compute_op=ALU.add).then_inc(added, 16)
                pool.wait_ge(added, 16 * (2 * i + q) + 16)
                pool.sem_inc(rows_free, 1)

            ix.wait()
            for i in range(2):
                gather(i, 0)
                gather(i, 1)
            pool.wait_ge(sums_in, 16 * (B + 1))
            before = ix.n
            with pool.Fori(0, NT // 2 - 1) as i:
                ix.before, ix.n = before + 4 * i, 0
                for q in range(2):
                    gather(i + 2, q)
                for q in range(2):
                    add_rows(i, q)
            ix.before, ix.n = before + 4 * (NT // 2 - 1), 0
            for j in range(NT - 3, NT):
                add_rows(j // 2, j % 2)

        @block.scalar
        def _(act):
            act.dma_start(bgb, bg.rearrange("(o n) -> o n", o=1).broadcast_to([P, NE])).then_inc(w_in, 16)
            for a, v in enumerate((lq1, lk1, lq2, lk2)):
                act.dma_start(lam_in[:, a, :], v.rearrange("(o n) -> o n", o=1).broadcast_to([P, HD])
                              ).then_inc(w_in, 16)
            for o, v in ((0, b1), (H, b2), (2 * H, b3)):
                act.dma_start(bias_in[0:NE, o:o + v.shape[1]], v).then_inc(w_in, 16)
            act.dma_start(wproj_sb[:, :, :], Wproj.rearrange("(k p) n -> p k n", p=P)).then_inc(w_in, 16)

            n = 0
            nv = 0

            def deviations(b):
                act.wait_ge(ve_ready, b + 1)
                act.activation(sd[:, b * KB:(b + 1) * KB], ve[:, b * KB:(b + 1) * KB], ACT.Sqrt
                               ).then_inc(sd_ready, 1)

            def copy_xnT(b):
                act.wait_ge(xnT_ps, b + 1)
                if b >= 2:
                    act.wait_ge(vg_ps, KB * (b - 1))
                for k in range(KC):
                    act.activation(xnT[:, b % 2, k, :], bank[k][:, :], ACT.Copy).then_inc(xnT_ready, 1)

            deviations(0)
            deviations(1)
            copy_xnT(0)
            for b in range(B):
                for f in range(4):
                    act.wait_ge(qk_ps, n + 1)
                    if n >= 2:
                        act.wait_ge(stacked[n % 2], 16 * 3 * (n // 2))
                    act.activation(parts[:, n % 2, 0, :], bank[2 + n % 2][:, :], ACT.Copy).then_inc(part0, 1)
                    n += 1
                if b + 1 < B:
                    copy_xnT(b + 1)
                if b + 2 < B:
                    deviations(b + 2)
                for k in range(KB):
                    act.wait_ge(vg_ps, nv + 1)
                    act.wait_ge(rings_set, 4)
                    act.activation(v_all[:, b * HG:(b + 1) * HG, k, :, 0:VD],
                                   bank[4 + nv % 2][:, 0:D].rearrange("p (g h e) -> p g h e", g=HG, h=4),
                                   ACT.Copy).then_inc(v_copied, 1)
                    nv += 1
            act.wait_ge(lam_ready, 1)
            act.activation(lam_e, lam_d, ACT.Exp).then_inc(lam_exp, 1)
            act.wait_ge(ex9_in, 1)
            act.activation(ex9, ex9, ACT.Exp).then_inc(ex9_out, 1)

            act.sem_inc(exp_done, 2)

            def copy_mT(i, r):
                act.wait_ge(mT_ps, 4 * i + r + 1)
                act.activation(mT[:, r % 2, :], bank[5][0:12, 0:T // 2].bitcast(BF16), ACT.Copy
                               ).then_inc(mT_ready, 1)

            def copy_outT(i, r):
                act.wait_ge(pv_done, KB * (4 * i + r) + KB)
                act.activation(outT[:, (r + 1) % 2, :], bank[4][:, :], ACT.Copy).then_inc(outT_ready, 1)

            copy_mT(0, 0)
            act.wait_ge(rt, RT_STEPS)
            act.wait_ge(slots_ready, 1)
            act.wait_ge(xn_saved, 16 * 2)
            act.wait_ge(bias_saved, 16)
            act.wait_ge(slot_zero, 16)
            act.wait_ge(minus_in, 16 * 4)
            for k in range(2):
                act.wait_ge(stacked[k], 16 * 3 * 8)
            assert UNITS // 4 == NE == (NE - late_experts) * KC and HC % 2 == 0

            def load_weights(i, r):
                if r < 2:
                    half = slice(r * HC // 2, (r + 1) * HC // 2)
                    act.dma_start(column(w2v, i)[:, half], row(W2.rearrange("e (k p) n -> e p k n", p=P), i)[:, half]
                                  ).then_inc(w12_in, 16)
                elif r == 2:
                    act.dma_start(column(w1_sb.rearrange("p (c n) -> p c n", n=H), i),
                                  row(W1.rearrange("e (k p) n -> (e k) p n", p=P), i)).then_inc(w12_in, 16)

            def step(i, r, tail):
                load_weights(i, r)
                copy_outT(i, r)
                for n, (kb, h0, heads, w) in enumerate(B_GROUPS):
                    act.wait_ge(st_ps, NG * (4 * i + r) + n + 1)
                    if n == 0 or B_GROUPS[n - 1][0] != kb:
                        act.wait_ge(pv_done, KB * (4 * i + r) + kb + 1)
                    src = B_BANKS[n % 2][:, 0:w * heads].rearrange("p (h n) -> p h n", h=heads)
                    act.activation(pt[kb][:, h0:h0 + heads, :], src, ACT.Exp, scale=SCALE
                                   ).then_inc(exp_done, 1)
                    if n == B_LAST[0] and not (tail and r == 3):
                        copy_mT(i + (r + 1) // 4, (r + 1) % 4)

            unit_loop(act, step)
            copy_outT(UNITS // 4, 0)

            act.wait_ge(ssq_ready, 1)
            act.activation(rms[:, :, :], ssq_b, ACT.Sqrt).then_inc(rms_ready, 1)
            for b in range(B):
                act.wait_ge(dT_ps, b + 1)
                if b >= 2:
                    act.wait_ge(proj_ps, KB * (b - 1))
                for k in range(KC):
                    act.activation(dT[b % 2][:, k, :], bank[4 * (b % 2) + k][:, :], ACT.Copy
                                   ).then_inc(dT_ready, 1)

            act.wait_ge(slots_in, 16)
            act.sem_inc(rows_free, 2)
            act.sem_inc(y_ready, 2)
            act.sem_inc(h_ready[1], 2)

            def gelu(layer, i, q):
                act.wait_ge(l_ps[layer], 2 * i + q + 1)
                act.activation(hbuf[:, q, :], bank[q][:, :], ACT.Gelu).then_inc(h_ready[layer], 1)

            def rows_out(i, q):
                act.wait_ge(y_ps, 2 * i + q + 1)
                act.wait_ge(rows_free, 2 * i + q + 1)
                act.activation(ybuf[:, q, :], bank[6 + q][:, 0:D], ACT.Copy,
                               scale=column(slot_sb, 2 * i + q)[:, 1:2]).then_inc(y_ready, 1)

            gelu(0, 0, 0)
            gelu(0, 0, 1)

            def experts(i, pair, tail):
                for q in pair:
                    gelu(1, i, q)
                for q in pair:
                    if not tail:
                        gelu(0, i + 1, q)
                    rows_out(i, q)

            tile_loop(act, experts)

        @block.vector
        def _(dve):
            st = Steps(dve, ln)
            n = 0
            nv = 0

            def norm(b):
                dve.wait_ge(x_in[b], 16)
                t0, t1 = b * KB, (b + 1) * KB
                for t in range(t0, t1):
                    st.done(dve.bn_stats(stats[:, t, :], x_all[:, t, :]))
                st.wait()
                for t in range(t0, t1):
                    st.done(dve.bn_aggr(mv[:, t, :], stats[:, t, :]))
                st.wait()
                dve.tensor_scalar(ve[:, t0:t1], mv[:, t0:t1, 1], EPS, None, ALU.add).then_inc(ve_ready, 1)
                dve.wait_ge(sd_ready, b + 1)
                st.then_wait(dve.reciprocal(rstd[:, t0:t1], sd[:, t0:t1]))
                st.then_wait(dve.tensor_tensor(nwt[:, t0:t1], rstd[:, t0:t1], rstd[:, t0:t1], ALU.mult))
                st.then_wait(dve.tensor_tensor(nwt[:, t0:t1], nwt[:, t0:t1], ve[:, t0:t1], ALU.mult))
                st.then_wait(dve.tensor_scalar(nwt[:, t0:t1], nwt[:, t0:t1], -0.5, 1.5, ALU.mult, ALU.add))
                st.then_wait(dve.tensor_tensor(rstd[:, t0:t1], rstd[:, t0:t1], nwt[:, t0:t1], ALU.mult))
                for t in range(t0, t1):
                    dve.tensor_scalar(xn_all[:, t, :], x_all[:, t, :], mv[:, t, 0:1], rstd[:, t:t + 1],
                                      ALU.subtract, ALU.mult).then_inc(xn_ready, 1)

            norm(0)
            norm(1)
            dve.wait_ge(w_in, W_IN)
            st.then_wait(dve.tensor_tensor(lam_pr, lam_in[:, 0:4:2, :], lam_in[:, 1:4:2, :], ALU.mult))
            dve.tensor_reduce(lam_d, lam_pr, X, ALU.add).then_inc(lam_ready, 1)
            for b in range(B):
                for f in range(4):
                    dve.wait_ge(part0, n + 1)
                    if n >= 2:
                        dve.wait_ge(part2, n - 1)
                    dve.tensor_tensor(rest[:, n % 2, :], bank[2 + n % 2][:, :], parts[:, n % 2, 0, :],
                                      ALU.subtract).then_inc(rest_ready, 1)
                    if n >= 2:
                        dve.wait_ge(stacked[n % 2], 16 * 3 * (n // 2))
                    dve.wait_ge(rest_ready, n + 1)
                    dve.tensor_copy(parts[:, n % 2, 1, :], rest[:, n % 2, :]).then_inc(part1, 1)
                    n += 1
                if b + 2 < B:
                    norm(b + 2)
                for k in range(KB):
                    dve.wait_ge(vg_ps, nv + 1)
                    dve.wait_ge(v_copied, nv + 1)
                    dve.tensor_tensor(logits[:, nv, :], bank[4 + nv % 2][:, D:D + NE], bgb, ALU.add
                                      ).then_inc(lg_ready, 1)
                    nv += 1

            s = Steps(dve, rt)
            do = s.then_wait

            def over_e(v):
                return v.unsqueeze(2).to_broadcast([P, TT, NE])

            def maxima(i, r, g):
                t, h0, heads, w = A_GROUPS[g]
                dve.wait_ge(s_ps, NG * (4 * i + r) + g + 1)
                src = A_BANKS[g % 3][:, 0:w * heads].rearrange("p (h n) -> p h n", h=heads)
                dve.tensor_reduce(mx[:, r % 2, h0:h0 + heads, t], src, X, ALU.max).then_inc(s_read, 1)

            def max_part(i, r, k):
                m, rr = mx[:, r % 2], mrest[:, r % 2]
                mp = mparts[:, r % 2].rearrange("p t h c -> p h t c")
                if k == 0:
                    dve.wait_ge(s_read, NG * (4 * i + r + 1) + 3)
                    dve.tensor_copy(mp[:, :, :, 0], m).then_inc(mx_step, 1)
                else:
                    dve.wait_ge(mx_step, 3 * (4 * i + r) + k)
                if k == 1:
                    dve.tensor_tensor(rr, m, mp[:, :, :, 0], ALU.subtract).then_inc(mx_step, 1)
                if k == 2:
                    dve.tensor_copy(mp[:, :, :, 1], rr).then_inc(mx_step, 1)
                if k == 3:
                    dve.tensor_tensor(mp[:, :, :, 2], rr, mp[:, :, :, 1], ALU.subtract).then_inc(mp_ready, 1)

            dve.sem_inc(s_read, 3)
            dve.wait_ge(lg_ready, TT)
            dve.wait_ge(consts, CONSTS)
            rev = rev8.unsqueeze(1).to_broadcast([P, TT, NE])
            for lg, m, w, oh in ((logits, m1, wm, oh1), (lg2, m2, wm2, oh2)):
                if lg is lg2:
                    do(dve.scalar_tensor_tensor(out=lg2, in0=oh1, scalar=NEG, in1=logits,
                                                op0=ALU.mult, op1=ALU.add))
                do(dve.tensor_reduce(m, lg, X, ALU.max))
                do(dve.tensor_tensor(eq, lg, over_e(m), ALU.is_equal))
                do(dve.tensor_tensor(eq, eq, rev, ALU.mult))
                do(dve.tensor_reduce(w, eq, X, ALU.max))
                do(dve.tensor_tensor(oh, eq, over_e(w), ALU.is_equal))
            dve.tensor_tensor(oh12, oh1, oh2, ALU.add).then_inc(oh_ready, 1)
            do(dve.tensor_tensor(ex9[:, :, 0:NE], logits, over_e(m1), ALU.subtract))
            dve.tensor_tensor(ex9[:, :, NE:9], m2.unsqueeze(2), m1.unsqueeze(2), ALU.subtract
                              ).then_inc(ex9_in, 1)
            for g in range(NG):
                maxima(0, 0, g)
            for k in range(4):
                max_part(0, 0, k)
            for g in range(NG):
                maxima(0, 1, g)
            dve.wait_ge(rank_ps, 2)
            do(dve.tensor_copy(cnt, bank[6][:, 0:NE]))
            do(dve.tensor_tensor(full, cnt.unsqueeze(2).to_broadcast([P, NE, TT]),
                                 thr.unsqueeze(1).to_broadcast([P, NE, TT]), ALU.is_gt))
            do(dve.tensor_reduce(ctile, full, X, ALU.add))
            do(dve.memset(base[:, 0:1], 0.0))
            for e in range(1, NE):
                do(dve.tensor_tensor(base[:, e:e + 1], base[:, e - 1:e], ctile[:, e - 1:e], ALU.add))
            do(dve.tensor_scalar(base128, base, float(P), None, ALU.mult))
            do(dve.tensor_tensor(pos, bank[4][:, 0:TT * NE].rearrange("p (t e) -> p t e", e=NE),
                                 base128.unsqueeze(1).to_broadcast([P, TT, NE]), ALU.add))
            for c, oh in enumerate((oh1, oh2)):
                do(dve.tensor_tensor(eq, pos, oh, ALU.mult))
                do(dve.tensor_reduce(slot_f[:, c * TT:(c + 1) * TT], eq, X, ALU.add))
            do(dve.tensor_copy(slots_i, slot_f))
            do(dve.tensor_scalar(slot_lo, slots_i, P - 1, None, ALU.bitwise_and))
            do(dve.tensor_scalar(slot_hi, slots_i, 7, None, ALU.logical_shift_right))
            do(dve.tensor_scalar(slot_lo, slot_lo, float(NT + 1), None, ALU.mult))
            dve.tensor_tensor(slot_at[:, :], slot_lo, slot_hi, ALU.add).then_inc(slots_ready, 1)
            do(dve.tensor_tensor(past, tile_no.unsqueeze(2).to_broadcast([P, NT + 1, NE - 1]),
                                 base[:, 1:NE].unsqueeze(1).to_broadcast([P, NT + 1, NE - 1]), ALU.is_ge))
            do(dve.tensor_reduce(texp_f, past, X, ALU.add))
            do(dve.tensor_copy(texp[:, :], texp_f))
            dve.wait_ge(ex9_out, 1)
            do(dve.tensor_reduce(esum, ex9[:, :, 0:NE], X, ALU.add))
            do(dve.reciprocal(wts[:, 0, :], esum))
            do(dve.tensor_tensor(wts[:, 1, :], ex9[:, :, NE], wts[:, 0, :], ALU.mult))
            dve.wait_ge(lam_exp, 1)
            do(dve.tensor_tensor(neglam[:, :], lam_e[:, 1:2], lam_e[:, 0:1], ALU.subtract))
            do(dve.tensor_scalar(neglam[:, :], neglam[:, :], -LAMBDA_INIT, None, ALU.add))
            do(dve.memset(bank[4][:, :], 1.0))
            do(dve.memset(a1[:, :, :], 0.0))
            dve.sem_inc(o_read, 1)
            assert s.n == RT_STEPS, s.n

            rows_of_bank = bank[6][:, :].rearrange("p (g e) -> p g e", e=32)

            def row_sums(i, r):
                dve.wait_ge(o_ps, 4 * i + r + 1)
                dve.reciprocal(rsum[:, r % 2, :], rows_of_bank[:, :, VD]).then_inc(at_step, 1)

            def normalize(i, r):
                rs = rsum[:, r % 2, :].unsqueeze(2).to_broadcast([P, 4 * KB, VD])
                o = rows_of_bank[:, :, 0:VD]
                dve.wait_ge(at_step, 4 * i + r + 1)
                if r % 2 == 0:
                    dve.scalar_tensor_tensor(out=a2[:, :, :], in0=o, scalar=neglam[:, 0:1], in1=rs,
                                             op0=ALU.mult, op1=ALU.mult).then_inc(o_read, 1)
                else:
                    dve.wait_ge(diff_done, 2 * i + r // 2 + 1)
                    dve.tensor_tensor(a1[:, :, :], o, rs, ALU.mult).then_inc(o_read, 1)

            def step(i, r, tail):
                ahead = not (tail and r >= 2)
                i1, r1 = i + (r + 1) // 4, (r + 1) % 4
                i2, r2 = i + (r + 2) // 4, (r + 2) % 4
                if not (tail and r == 3):
                    dve.wait_ge(mT_ps, 4 * i + r + 1)
                for g in range(NG):
                    if g < 4 and not (tail and r == 3):
                        max_part(i1, r1, g)
                    if g == 7:
                        row_sums(i, r)
                    if g == 8:
                        normalize(i, r)
                    if ahead:
                        maxima(i2, r2, g)

            unit_loop(dve, step)
            row_sums(UNITS // 4, 0)
            normalize(UNITS // 4, 0)

            e = Steps(dve, ep)
            dve.wait_ge(ssq_done, 2 * (UNITS // 4) + 1)
            dve.tensor_scalar(ssq_b, ssq_b, 1.0 / VD, EPS, ALU.mult, ALU.add).then_inc(ssq_ready, 1)
            dve.wait_ge(rms_ready, 1)
            c = 1.0 - LAMBDA_INIT
            for b in range(B):
                e.then_wait(dve.reciprocal(rinv[:, b, :], rms[:, b, :]))
                e.then_wait(dve.tensor_tensor(rms[:, b, :], rinv[:, b, :], rinv[:, b, :], ALU.mult))
                e.then_wait(dve.tensor_tensor(rms[:, b, :], rms[:, b, :], ssq_b[:, b, :], ALU.mult))
                e.then_wait(dve.tensor_scalar(rms[:, b, :], rms[:, b, :], -0.5 * c, 1.5 * c, ALU.mult, ALU.add))
                dve.tensor_tensor(rinv[:, b, :], rinv[:, b, :], rms[:, b, :], ALU.mult).then_inc(norms_ready, 1)
                dve.wait_ge(norms_ready, b + 1)
                scale_pair(dve, b, 0).then_inc(dn_ready[0], 1)
            for tt in range(TT):
                dve.wait_ge(proj_ps, tt + 1)
                dve.tensor_tensor(x_all[:, tt, :], x_all[:, tt, :], bank[2 + tt % 2][:, 0:D], ALU.add
                                  ).then_inc(proj_read, 1)

            def copy_xT(i, q):
                dve.wait_ge(xT_ps, 2 * i + q + 1 + 2)
                dve.tensor_copy(xT[:, q, :, :], bank[4 + q][:, 0:KC * P].rearrange(
                    "p (k n) -> p k n", k=KC)).then_inc(xT_ready, 1)

            def copy_hT(layer, i, q):
                dve.wait_ge(hT_ps[layer], 2 * i + q + 1)
                dve.tensor_copy(hT[:, q, :, :], bank[2 + q][:, :].rearrange("p (k n) -> p k n", k=HC)
                                ).then_inc(hT_ready[layer], 1)

            def experts(i, pair, tail):
                for q in pair:
                    copy_hT(0, i, q)
                    if not tail:
                        dve.wait_ge(l_ps[0], 2 * i + q + 1)
                        copy_xT(i + 1, q)
                for q in pair:
                    copy_hT(1, i, q)

            dve.sem_inc(hT_ready[1], 2)
            copy_xT(0, 0)
            copy_xT(0, 1)
            tile_loop(dve, experts)

        @block.tensor
        def _(pe):
            pe.wait_ge(w_in, W_IN)
            pe.wait_ge(consts, CONSTS)
            pe.sem_inc(pv_done, KB)
            pe.sem_inc(xT_ps, 2)

            def transposes(b):
                pe.wait_ge(xn_ready, KB * (b + 1))
                if b > 0:
                    pe.wait_ge(xnT_ready, KC * b)
                for k in range(KC):
                    for t in range(KB):
                        mm = pe.transpose(bank[k][:, t * P:(t + 1) * P],
                                          xn_all[:, b * KB + t, k * P:(k + 1) * P], ident[:, :])
                mm.then_inc(xnT_ps, 1)

            n = 0
            nv = 0
            transposes(0)
            for b in range(B):
                pe.wait_ge(xnT_ready, KC * (b + 1))
                for f in range(4):
                    if n >= 2:
                        pe.wait_ge(rest_ready, n - 1)
                    for k in range(KC):
                        mm = pe.matmul(bank[2 + n % 2][:, :], wqk[:, k, f * P:(f + 1) * P], xnT[:, b % 2, k, :],
                                       start=(k == 0), stop=(k == KC - 1))
                    mm.then_inc(qk_ps, 1)
                    n += 1
                if b + 1 < B:
                    transposes(b + 1)
                for t in range(KB):
                    if nv >= 2:
                        pe.wait_ge(lg_ready, nv - 1)
                    for k in range(KC):
                        mm = pe.matmul(bank[4 + nv % 2][:, 0:D + NE], xnT[:, b % 2, k, t * P:(t + 1) * P],
                                       wvg[:, k, :], start=(k == 0), stop=(k == KC - 1))
                    mm.then_inc(vg_ps, 1)
                    nv += 1

            def scores(i, r, g):
                t, h0, heads, w = A_GROUPS[g]
                if g == 0:
                    pe.wait_ge(unit_in[r], 16 * 4 * (i + 1))
                pe.wait_ge(s_read, NG * (4 * i + r) + g + 1)
                for c in range(heads):
                    o = A_BANKS[g % 3][:, c * w:(c + 1) * w]
                    pe.matmul(o, q_ring[0:MAX_AT, r, h0 + c, t * P:(t + 1) * P],
                              k_ring[0:MAX_AT, r, (h0 + c) % 2, 0:w], start=True, stop=False)
                    mm = pe.matmul(o[:, t * P:(t + 1) * P], identb[:, :], causal[:, :], start=False, stop=True)
                mm.then_inc(s_ps, 1)

            def scores_T(i, r, g):
                kb, h0, heads, w = B_GROUPS[g]
                if g == 0:
                    pe.wait_ge(max_rows[r], 16 * 4 * (i + 1))
                pe.wait_ge(exp_done, NG * (4 * i + r) + g + 1)
                for c in range(heads):
                    mm = pe.matmul(B_BANKS[g % 2][:, c * w:(c + 1) * w],
                                   k_ring[:, r, (h0 + c) % 2, kb * P:(kb + 1) * P],
                                   q_ring[:, r, h0 + c, kb * P:T], start=True, stop=True)
                mm.then_inc(st_ps, 1)

            def values(i, r, kb):
                if kb == 0:
                    pe.wait_ge(outT_ready, 4 * i + r + 1)
                    pe.wait_ge(v_ready, 2 * i + r // 2 + 1)
                pe.wait_ge(masked, KB * (4 * i + r) + kb + 1)
                for hh in range(4):
                    mm = pe.matmul(bank[4][32 * hh:32 * hh + 32, kb * P:T], v_unit[:, r // 2, kb, hh, :],
                                   pt[kb][:, hh, :], start=(kb == 0), stop=(kb == KB - 1),
                                   skip_group_check=True)
                mm.then_inc(pv_done, 1)

            def turn_rows(i, r):
                pe.wait_ge(outT_ready, 4 * i + r + 1)
                pe.wait_ge(o_read, 4 * i + r + 1)
                for t in range(KB):
                    mm = pe.transpose(bank[6][:, t * P:(t + 1) * P], outT[:, (r + 1) % 2, t * P:(t + 1) * P],
                                      ident[:, :])
                mm.then_inc(o_ps, 1)

            def turn_max(i, r, first=False):
                pe.wait_ge(mp_ready, 4 * i + r + 1)
                if not first:
                    pe.wait_ge(mT_ready, 4 * i + r)
                for t in range(KB):
                    mm = pe.transpose(bank[5][0:12, t * P // 2:(t + 1) * P // 2].bitcast(BF16),
                                      mparts[:, r % 2, t, :, :].rearrange("p h c -> p (h c)"), identb[:, :])
                mm.then_inc(mT_ps, 1)

            def ranks():
                pe.wait_ge(oh_ready, 1)
                mm = pe.matmul(bank[4][:, 0:TT * NE], below[:, :], oh12.rearrange("p t e -> p (t e)"),
                               start=True, stop=False, skip_group_check=True)
                for t in range(TT - 1):
                    mm = pe.matmul(bank[4][:, (t + 1) * NE:TT * NE].rearrange("p (t e) -> p t e", e=NE), onesb[:, :],
                                   oh12[:, t:t + 1, :].to_broadcast([P, TT - 1 - t, NE]),
                                   start=False, stop=(t == TT - 2), skip_group_check=True)
                mm.then_inc(rank_ps, 1)
                for t in range(TT):
                    mm = pe.matmul(bank[6][:, 0:NE], onesb[:, :], oh12[:, t, :], start=(t == 0), stop=(t == TT - 1))
                mm.then_inc(rank_ps, 1)

            for g in range(NG):
                scores(0, 0, g)
            ranks()
            turn_max(0, 0, first=True)
            for g in range(NG):
                scores(0, 1, g)

            def step(i, r, tail):
                ahead = not (tail and r >= 2)
                a = iter(range(NG))

                def next_scores(count=1):
                    if ahead:
                        for _ in range(count):
                            scores(i + (r + 2) // 4, (r + 2) % 4, next(a))

                for g in range(4):
                    next_scores()
                    scores_T(i, r, g)
                turn_rows(i, r)
                if not (tail and r == 3):
                    turn_max(i + (r + 1) // 4, (r + 1) % 4)
                for g in range(4, 7):
                    next_scores()
                    scores_T(i, r, g)
                scores_T(i, r, 7)
                values(i, r, 0)
                for g in range(8, 10):
                    scores_T(i, r, g)
                next_scores()
                values(i, r, 1)
                for g in range(10, 12):
                    scores_T(i, r, g)
                next_scores(2)
                values(i, r, 2)
                next_scores(2)
                values(i, r, 3)

            unit_loop(pe, step)
            turn_rows(UNITS // 4, 0)

            def turn_differences(b):
                for k in range(KC):
                    pe.wait_ge(dn_ready[k], b + 1)
                    if b >= 2:
                        pe.wait_ge(dT_ready, KC * (b - 1))
                    for t in range(KB):
                        mm = pe.transpose(bank[4 * (b % 2) + k][:, t * P:(t + 1) * P],
                                          d_all[:, 1 + b * HG // 2 + k, t].rearrange("p s n -> p (s n)"),
                                          ident[:, :])
                mm.then_inc(dT_ps, 1)

            turn_differences(0)
            for b in range(B):
                if b + 1 < B:
                    turn_differences(b + 1)
                pe.wait_ge(dT_ready, KC * (b + 1))
                for t in range(KB):
                    tt = b * KB + t
                    if tt >= 2:
                        pe.wait_ge(proj_read, tt - 1)
                    for k in range(KC):
                        mm = pe.matmul(bank[2 + tt % 2][:, 0:D], dT[b % 2][:, k, t * P:(t + 1) * P],
                                       wproj_sb[:, k, :], start=(k == 0), stop=(k == KC - 1))
                    mm.then_inc(proj_ps, 1)

            pe.wait_ge(proj_read, TT)
            pe.wait_ge(w12_in, 16 * 3 * (UNITS // 4))
            pe.wait_ge(w3_in, 16 * (NE + late_experts))
            pe.wait_ge(bias_in_sb, 16)
            BW = 2 * H + D

            def expert_of(i, q):
                j = 2 * i + q
                col = texp[0:1, j:j + 1] if isinstance(j, int) else texp[0:1, bass.ds(j, 1)]
                return pe.value_load(col, min_val=0, max_val=NE - 1)

            def turn_x(i, q):
                pe.wait_ge(gathered[q], 16 * (i + 1))
                for k in range(KC):
                    mm = pe.transpose(bank[4 + q][:, k * P:(k + 1) * P], xg[:, q, k * P:(k + 1) * P], ident[:, :])
                mm.then_inc(xT_ps, 1)

            def layer(o, e, rows, chunks, w, width, bias_at):
                pe.matmul(o, onesb[0:3, :], bias_sb[:, bass.ds(e * BW + bias_at, width)], start=True, stop=False)
                for k in range(chunks):
                    mm = pe.matmul(o, rows[:, k, :], w[:, bass.ds((e * chunks + k) * width, width)],
                                   start=False, stop=(k == chunks - 1))
                return mm

            def layer1(i, q):
                e = expert_of(i, q)
                pe.wait_ge(xT_ready, 2 * i + q + 1)
                pe.wait_ge(h_ready[1], 2 * i + q + 1)
                layer(bank[q][:, :], e, xT[:, q], KC, w1_sb, H, 0).then_inc(l_ps[0], 1)

            def layer2(i, q, e):
                pe.wait_ge(hT_ready[0], 2 * i + q + 1)
                layer(bank[q][:, :], e, hT[:, q], HC, w2_sb, H, H).then_inc(l_ps[1], 1)

            def layer3(i, q, e):
                pe.wait_ge(hT_ready[1], 2 * i + q + 1 + 2)
                pe.wait_ge(y_ready, 2 * i + q + 1)
                layer(bank[6 + q][:, 0:D], e, hT[:, q], HC, w3_sb, D, 2 * H).then_inc(y_ps, 1)

            def turn_h(layer, i, q):
                pe.wait_ge(h_ready[layer], 2 * i + q + 1 + (2 if layer else 0))
                if layer == 0:
                    pe.wait_ge(hT_ready[1], 2 * i + q + 1)
                for k in range(HC):
                    mm = pe.transpose(bank[2 + q][:, k * P:(k + 1) * P], hbuf[:, q, k * P:(k + 1) * P], ident[:, :])
                mm.then_inc(hT_ps[layer], 1)

            turn_x(0, 0)
            turn_x(0, 1)
            layer1(0, 0)
            layer1(0, 1)

            def experts(i, pair, tail):
                for q in pair:
                    turn_h(0, i, q)
                    if not tail:
                        turn_x(i + 1, q)
                e = [expert_of(i, q) for q in pair]
                for q in pair:
                    layer2(i, q, e[q])
                turn_h(1, i, 0)
                if not tail:
                    layer1(i + 1, 0)
                    turn_h(1, i, 1)
                layer3(i, 0, e[0])
                if not tail:
                    layer1(i + 1, 1)
                    layer3(i, 1, e[1])

            tile_loop(pe, experts)


_INS = ['L0_attn_x', 'L0_attn_Wqkv', 'L0_attn_Wproj', 'L0_attn_lambda_q1', 'L0_attn_lambda_k1',
        'L0_attn_lambda_q2', 'L0_attn_lambda_k2', 'L0_ffn_W1', 'L0_ffn_b1', 'L0_ffn_W2', 'L0_ffn_b2',
        'L0_ffn_W3', 'L0_ffn_b3', 'L0_ffn_Wg', 'L0_ffn_bg']


def kernel(**inputs):
    import numpy as _np
    import concourse.bacc as _bacc
    from concourse import mybir as _mybir
    from concourse.bass_utils import run_bass_kernel_spmd as _run

    nc = _bacc.Bacc("TRN2", target_bir_lowering=False, num_devices=1)
    arrays, args = {}, []
    for name in _INS:
        a = _np.ascontiguousarray(inputs[name])
        arrays[f"in_{name}"] = a
        args.append(nc.dram_tensor(f"in_{name}", a.shape, _mybir.dt.from_np(a.dtype), kind="ExternalInput").ap())
    shape = inputs['L0_attn_x'].shape
    args.append(nc.dram_tensor("out_0", shape, _mybir.dt.float32, kind="ExternalOutput").ap())
    build(nc, *args)
    r = _run(nc, [arrays], core_ids=[0])
    return r.results[0]["out_0"]
```

```python
import math
from contextlib import ExitStack

import numpy as np

import concourse.bass as bass
from concourse import mybir

ALU = mybir.AluOpType
ACT = mybir.ActivationFunctionType
F32 = mybir.dt.float32
BF16 = mybir.dt.bfloat16
I32 = mybir.dt.int32
X = mybir.AxisListType.X

P = 128
EPS = 1e-5
NEG = -1e30


class Steps:

    def __init__(self, eng, sem):
        self.eng, self.sem, self.n, self.before = eng, sem, 0, 0

    def done(self, ins):
        ins.then_inc(self.sem, 1)
        self.n += 1

    def wait(self):
        self.eng.wait_ge(self.sem, self.before + self.n)

    def then_wait(self, ins):
        self.done(ins)
        self.wait()


def build(nc, x, Wqkv, Wproj, lq1, lk1, lq2, lk2, W1, b1, W2, b2, W3, b3, Wg, bg, out):
    B, T, D = x.shape
    NE, _, H = W1.shape
    N = B * T
    TT = N // P
    KB = T // P
    NH, HD, VD = 16, 8, 16
    KC = D // P
    HC = H // P
    HG = NH // 4
    GROUPS = 6
    STACK = GROUPS * HD
    MAX_AT = P - 3
    NT = (2 * N) // P + NE - 1
    UNITS = B * HG * 2
    LAMBDA_INIT = 0.8 - 0.6 * math.exp(-0.3)
    SCALE = 1.0 / math.sqrt(HD)
    VW = VD + 1
    Q_IN = (slice(0, 3), slice(3, 5), slice(5, 6))
    K_IN = (slice(1, 6, 2), slice(0, 5, 4), slice(2, 3))

    def scratch(name, shape, dtype):
        return nc.dram_tensor(name, shape, dtype).ap()

    q_stack = scratch("q_stack", [2, B * NH, HD, GROUPS, T], BF16)
    k_stack = scratch("k_stack", [2, B * NH, HD, GROUPS, T], BF16)
    xn_rows = scratch("xn_rows", [N + P, D], F32)
    slot_rows = scratch("slot_rows", [P * (NT + 1), 2], F32)
    sums = scratch("sums", [N + P, D], F32)
    bias_rows = scratch("bias_rows", [3, NE, D], BF16)

    with ExitStack() as ctx:
        def sb(name, shape, dt):
            return ctx.enter_context(nc.sbuf_tensor(name, shape, dt))

        def sem(name):
            return ctx.enter_context(nc.semaphore(name))

        bank = [ctx.enter_context(nc.psum_tensor(f"bank{k}", [P, 512], F32)) for k in range(8)]

        W12 = NE * (KC + HC) * H
        big = sb("big", [P, W12], F32)
        w1_sb = big[:, 0:NE * KC * H]
        w2_sb = big[:, NE * KC * H:W12]
        q_words = 4 * 4 * T // 2
        late_experts = q_words // (KC * H)
        assert late_experts * KC * H == q_words
        q_at = (NE - late_experts) * KC * H
        q_ring = big[:, q_at:q_at + q_words].bitcast(BF16).rearrange("p (r h n) -> p r h n", r=4, h=4)
        taken = [0]

        def in_big(n, dtype=F32):
            words = n if dtype in (F32, I32) else n // 2
            v = big[:, taken[0]:taken[0] + words]
            taken[0] += words
            return v if dtype == F32 else v.bitcast(dtype)

        xn_all = in_big(TT * D).rearrange("p (t d) -> p t d", t=TT)
        assert taken[0] <= q_at
        taken[0] = q_at + q_words
        xnT = in_big(2 * KC * T).rearrange("p (r k n) -> p r k n", r=2, k=KC)
        wqk = in_big(KC * 2 * D).rearrange("p (k n) -> p k n", k=KC)
        wvg = in_big(KC * (D + NE)).rearrange("p (k n) -> p k n", k=KC)
        rest = in_big(2 * T).rearrange("p (r n) -> p r n", r=2)
        parts = in_big(4 * 3 * T, BF16).rearrange("p (r c n) -> p r c n", r=4, c=3)
        stats = in_big(TT * 6).rearrange("p (t s) -> p t s", s=6)
        mv = in_big(TT * 2).rearrange("p (t s) -> p t s", s=2)
        ve = in_big(TT)
        sd = in_big(TT)
        rstd = in_big(TT)
        nwt = in_big(TT)
        route = [in_big(TT * NE).rearrange("p (t e) -> p t e", e=NE) for _ in range(6)]
        logits, eq, oh1, oh2, lg2, pos = route
        ex9 = in_big(TT * 9).rearrange("p (t e) -> p t e", e=9)
        oh12 = in_big(TT * NE, BF16).rearrange("p (t e) -> p t e", e=NE)
        small = [in_big(TT) for _ in range(6)]
        m1, wm, m2, wm2, esum, w2u = small
        rev8 = in_big(NE)
        thr = in_big(TT)
        bgb = in_big(NE)
        cnt = in_big(NE)
        full = in_big(NE * TT).rearrange("p (e j) -> p e j", e=NE)
        ctile = in_big(NE)
        base = in_big(NE)
        base128 = in_big(NE)
        tile_no = in_big(NT + 1)
        past = in_big((NT + 1) * (NE - 1)).rearrange("p (j e) -> p j e", j=NT + 1)
        texp_f = in_big(NT + 1)
        slot_f = in_big(2 * TT)
        slot_lo = in_big(2 * TT, I32)
        slot_hi = in_big(2 * TT, I32)
        slots_i = in_big(2 * TT, I32)
        no_slot = in_big(2 * (NT + 1)).rearrange("p (j c) -> p j c", c=2)
        lam_in = in_big(4 * HD).rearrange("p (a d) -> p a d", a=4)
        lam_pr = in_big(2 * HD).rearrange("p (a d) -> p a d", a=2)
        lam_d = in_big(2)
        lam_e = in_big(2)
        bias_in = in_big(D)
        bias_r = in_big(D)
        bias_p = in_big(3 * D, BF16).rearrange("p (c n) -> p c n", c=3)
        minus1 = in_big(2 * T, BF16)
        assert taken[0] <= W12

        x_all = sb("x_all", [P, TT, D], F32)
        d_all = sb("d_all", [P, 1 + B * HG // 2, KB, 2, 4 * VD], F32)
        slot_at = sb("slot_at", [P, 2 * TT], I32)
        pairs = sb("pairs", [P, 2 * TT, 2], F32)
        wts = pairs[:, :, 1].rearrange("p (c t) -> p c t", c=2)
        at_now = sb("at_now", [P, 4, 1], I32)
        pair_now = sb("pair_now", [P, 4, 2], F32)
        texp = sb("texp", [P, NT + 1], I32)
        slot_sb = sb("slot_sb", [P, NT + 1, 2], F32)
        neglam = sb("neglam", [P, 1], F32)
        b12 = sb("b12", [2 * NE * HC, P], F32)
        b12T = sb("b12T", [P, 2 * NE * HC], F32)
        wproj_sb = sb("wproj_sb", [P, KC, D], F32)
        ident = sb("ident", [P, P], F32)
        identb = sb("identb", [P, P], BF16)
        causal = sb("causal", [P, P], BF16)
        below = sb("below", [P, P], BF16)
        onesb = sb("onesb", [P, P], BF16)

        half = 4 * 2 * T // 2
        pt_at = [4 * sum(T - P * j for j in range(kb)) for kb in range(KB + 1)]
        shared = sb("shared", [P, max(NE * HC * D, half + pt_at[KB])], F32)
        w3_sb = shared[:, 0:NE * HC * D]
        k_ring = shared[:, 0:half].bitcast(BF16).rearrange("p (r j n) -> p r j n", r=4, j=2)
        pt = [shared[:, half + pt_at[kb]:half + pt_at[kb + 1]].rearrange("p (h n) -> p h n", h=4)
              for kb in range(KB)]
        v_words = B * HG * KB * 4 * VW
        vbuf = sb("vbuf", [P, v_words + 2 * KB * 4 * 32], F32)
        v_all = vbuf[:, 0:v_words].rearrange("p (g k h e) -> p g k h e", g=B * HG, k=KB, h=4)
        v_unit = vbuf[:, v_words:v_words + 2 * KB * 4 * 32].rearrange(
            "p (r k h e) -> p r k h e", r=2, k=KB, h=4)
        b3_sb = vbuf[0:3, 0:NE * D // 2].bitcast(BF16)
        assert NE * D // 2 <= v_words + 2 * KB * 4 * 32
        mx = sb("mx", [P, 2, 4, KB], F32)
        mrest = sb("mrest", [P, 2, 4, KB], F32)
        mparts = sb("mparts", [P, 2, KB, 3, 4], BF16)
        mT = sb("mT", [12, 2, T], BF16)
        outT = sb("outT", [P, 2, T], F32)
        dT_b = sb("dT_b", [P, KC, T], F32)
        rsum = sb("rsum", [P, 2, 4 * KB], F32)
        a1 = sb("a1", [P, 4 * KB, VD], F32)
        a2 = sb("a2", [P, 4 * KB, VD], F32)
        squares = sb("squares", [P, KB, 4 * VD], F32)
        ssq = sb("ssq", [P, 1 + B * HG // 2, KB, 2, 4], F32)
        ssq_b = ssq[:, 1:].rearrange("p (b g) t s h -> p b (g t s h)", b=B)
        rms = sb("rms", [P, B, HG * KB * 4], F32)
        rinv = sb("rinv", [P, B, HG * KB * 4], F32)
        xg = sb("xg", [P, 2, D], F32)
        freed = d_all[:, :, :, :, :].rearrange("p g t s n -> p (g t s n)")
        hT = [freed[:, l * 2 * H:(l + 1) * 2 * H].rearrange("p (q k n) -> p q k n", q=2, k=HC)
              for l in range(2)]
        xT = freed[:, 4 * H:4 * H + 2 * D].rearrange("p (q k n) -> p q k n", q=2, k=KC)
        ybuf = freed[:, 4 * H + 2 * D:4 * H + 4 * D].rearrange("p (q n) -> p q n", q=2)
        assert KC * H == KC * T and 2 * HC * H <= TT * D
        w1_now = [v[:, :, :].rearrange("p k n -> p (k n)") for v in (outT, dT_b)]
        w2_now = x_all[:, :, :].rearrange("p t d -> p (t d)")[:, 0:2 * HC * H].rearrange(
            "p (q n) -> p q n", q=2)
        token_i = sb("token_i", [P, NT + 1], I32)
        idx = sb("idx", [P, 3, 1], I32)

        x_in = [sem(f"x_in{b}") for b in range(B)]
        w_in = sem("w_in")
        consts = sem("consts")
        ln = sem("ln")
        ve_ready = sem("ve_ready")
        sd_ready = sem("sd_ready")
        xn_ready = sem("xn_ready")
        xnT_ps = sem("xnT_ps")
        xnT_ready = sem("xnT_ready")
        qk_ps = sem("qk_ps")
        part0 = sem("part0")
        rest_ready = sem("rest_ready")
        part1 = sem("part1")
        part2 = sem("part2")
        stacked = [sem(f"stacked{k}") for k in range(4)]
        vg_ps = sem("vg_ps")
        v_copied = sem("v_copied")
        lg_ready = sem("lg_ready")
        rt = sem("rt")
        ex9_in = sem("ex9_in")
        ex9_out = sem("ex9_out")
        oh_ready = sem("oh_ready")
        rank_ps = sem("rank_ps")
        slots_ready = sem("slots_ready")
        lam_ready = sem("lam_ready")
        lam_exp = sem("lam_exp")
        bias_step = sem("bias_step")
        bias_parts = sem("bias_parts")
        bias_saved = sem("bias_saved")
        xn_saved = sem("xn_saved")
        slot_zero = sem("slot_zero")
        scattered = [sem(f"scattered{k}") for k in range(4)]
        w12_in = sem("w12_in")
        rings_set = sem("rings_set")
        minus_in = sem("minus_in")
        unit_in = [sem(f"unit_in{r}") for r in range(4)]
        max_rows = [sem(f"max_rows{r}") for r in range(4)]
        s_ps = sem("s_ps")
        s_read = sem("s_read")
        mx_step = sem("mx_step")
        mp_ready = sem("mp_ready")
        st_ps = sem("st_ps")
        exp_done = sem("exp_done")
        masked = sem("masked")
        v_ready = sem("v_ready")
        pv_done = sem("pv_done")
        outT_ready = sem("outT_ready")
        at_step = sem("at_step")
        ep = sem("ep")
        ssq_ready = sem("ssq_ready")
        rms_ready = sem("rms_ready")
        dn_ready = [sem("dn_ready0"), sem("dn_ready1")]
        dT_ps = sem("dT_ps")
        dT_ready = sem("dT_ready")
        proj_ps = sem("proj_ps")
        proj_read = sem("proj_read")
        w3_in = sem("w3_in")
        b3_in = sem("b3_in")
        idx_ready = sem("idx_ready")
        gathered = [sem("gathered0"), sem("gathered1")]
        xT_ps = sem("xT_ps")
        xT_ready = sem("xT_ready")
        l_ps = [sem("l1_ps"), sem("l2_ps")]
        h_ready = [sem("h1_ready"), sem("h2_ready")]
        w_ready = [sem("w1_ready"), sem("w2_ready")]
        b12T_ps = sem("b12T_ps")
        b12T_ready = sem("b12T_ready")
        y_ps = sem("y_ps")
        y_ready = sem("y_ready")
        added = sem("added")
        rows_free = sem("rows_free")
        sums_in = sem("sums_in")
        pool_on = sem("pool_on")
        pool_step = sem("pool_step")
        diff_done = sem("diff_done")
        ssq_done = sem("ssq_done")
        norms_ready = sem("norms_ready")
        slots_in = sem("slots_in")
        out_saved = sem("out_saved")

        dT = (outT, dT_b)
        xv = x.rearrange("b (k p) d -> b p k d", p=P)

        def groups_of(width):
            gs = []
            for t in range(KB):
                heads = min(4, 512 // width(t))
                gs += [(t, h, heads, width(t)) for h in range(0, 4, heads)]
            return gs

        A_GROUPS = groups_of(lambda t: P * (t + 1))
        B_GROUPS = groups_of(lambda t: T - P * t)
        NG = len(A_GROUPS)
        assert len(B_GROUPS) == NG
        ORDER = "AABABABmBABoBBAAVABVAABABVBV"
        OUT_AT = 3
        B_AHEAD = 3
        assert ORDER.count("A") == ORDER.count("B") == NG
        A_BANKS, B_BANKS = (bank[0], bank[1], bank[7]), (bank[2], bank[3], bank[5])
        V_BANKS = (bank[4], bank[6])
        NS = NG + 1
        O_AT = ORDER[:ORDER.index("o")].count("A")
        M_AT = ORDER[:ORDER.index("m")].count("B") + B_AHEAD
        assert NS % 3 == 0 and 2 < O_AT < NG and 2 < M_AT < NG

        EARLY = [range(f * NG // 4, (f + 1) * NG // 4) for f in range(4)]

        def a_place(g):
            return g if g < O_AT else g + 1

        def b_place(g):
            return g if g < M_AT else g + 1

        B_LAST = [max(n for n, g in enumerate(B_GROUPS) if g[0] == kb) for kb in range(KB)]

        def unit_loop(eng, body):
            with eng.Fori(0, UNITS // 4 - 1) as i:
                for r in range(4):
                    body(i, r, False)
            for r in range(4):
                body(UNITS // 4 - 1, r, True)

        assert NT % 2 == 1

        def tile_loop(eng, body):
            with eng.Fori(0, NT // 2 - 1) as i:
                body(i, (0, 1), (0, 1))
            body(NT // 2 - 1, (0, 1), (0,))
            body(NT // 2, (0,), ())

        def expert_of(eng, i, q):
            j = 2 * i + q
            col = texp[0:1, j:j + 1] if isinstance(j, int) else texp[0:1, bass.ds(j, 1)]
            return eng.value_load(col, min_val=0, max_val=NE - 1)

        def scale_pair(eng, b, k):
            d = d_all[:, 1 + b * HG // 2 + k].rearrange("p t s (h e) -> p (t s h) e", e=VD)
            return eng.tensor_tensor(d, d, rinv[:, b, k * 8 * KB:(k + 1) * 8 * KB].unsqueeze(2).to_broadcast(
                [P, 8 * KB, VD]), ALU.mult)

        def row(v, j):
            if isinstance(j, int):
                return v[j]
            names = "abcd"[:len(v.shape) - 2]
            return v[bass.ds(j, 1)].rearrange(f"o y {' '.join(names)} -> (o y) {' '.join(names)}")

        def column(v, j):
            if isinstance(j, int):
                return v[:, j]
            names = "abcd"[:len(v.shape) - 3]
            return v[:, bass.ds(j, 1)].rearrange(f"p o y {' '.join(names)} -> p (o y) {' '.join(names)}")

        W_IN = 16 * (3 + 1 + 4 + 3 + 1)
        CONSTS = 17
        RT_STEPS = 43

        block = ctx.enter_context(nc.Block())

        w1v = w1_sb.rearrange("p (e k n) -> p e k n", e=NE, k=KC)
        w2v = w2_sb.rearrange("p (e k n) -> p e k n", e=NE, k=HC)

        @block.sync
        def _(sp):
            for b in range(B):
                sp.dma_start(x_all[:, b * KB:(b + 1) * KB, :], xv[b]).then_inc(x_in[b], 16)
                if b == 0:
                    wq = Wqkv.rearrange("(k p) n -> p k n", p=P)
                    sp.dma_start(wqk, wq[:, :, 0:2 * D]).then_inc(w_in, 16)
                    sp.dma_start(wvg[:, :, 0:D], wq[:, :, 2 * D:3 * D]).then_inc(w_in, 16)
                    sp.dma_start(wvg[:, :, D:D + NE], Wg.rearrange("(k p) n -> p k n", p=P)
                                 ).then_inc(w_in, 16)
            def load(i, r):
                if not (isinstance(i, int) and 4 * i + r < 3):
                    sp.wait_ge(exp_done, NS * (4 * i + r - 2) + 3)
                def heads(stack, s):
                    return row(stack[r % 2].rearrange("(g s j) d c n -> s g (d c) j n", s=2, j=2)[s],
                               2 * i + r // 2)

                for s in range(2):
                    rows = slice(STACK * s, STACK * (s + 1))
                    sp.dma_start(q_ring[rows, r, 2 * s:2 * s + 2, :], heads(q_stack, s)
                                 ).then_inc(unit_in[r], 16)
                    sp.dma_start(k_ring[rows, r, :, :], heads(k_stack, s)).then_inc(unit_in[r], 16)

            def put_max(i, r):
                sp.wait_ge(exp_done, NS * (4 * i + r) + M_AT + 1 + 3)
                sp.dma_start(q_ring[MAX_AT:P, r, :, :], mT[:, r % 2, :]).then_inc(max_rows[r], 16)

            n = 0
            for b in range(B):
                for f in range(4):
                    stack = (q_stack, k_stack)[f % 2][f // 2][b * NH:(b + 1) * NH]
                    stack = stack.rearrange("h d g n -> (h d) g n")
                    for c, ready in enumerate((part0, part1, part2)):
                        sp.wait_ge(ready, n + 1)
                        to = stack[:, (Q_IN, K_IN)[f % 2][c]]
                        sp.dma_start(to, parts[:, n % 4, c, :].unsqueeze(1).to_broadcast(list(to.shape))
                                     ).then_inc(stacked[n % 4], 16)
                    n += 1
                if b == 1:
                    for k in range(4):
                        sp.wait_ge(stacked[k], 16 * 3 * 2)
                    sp.wait_ge(minus_in, 16 * 4)
                    sp.wait_ge(rings_set, 2)
                    for u in range(3):
                        load(0, u)
            put_max(0, 0)
            sp.wait_ge(xn_ready, TT)
            sp.dma_start(xn_rows[N:], xn_all[:, 0, :]).then_inc(xn_saved, 16)
            sp.dma_start(xn_rows[0:N].rearrange("(t p) d -> p t d", p=P), xn_all).then_inc(xn_saved, 16)
            for k in range(4):
                sp.wait_ge(stacked[k], 16 * 3 * B)
            sp.wait_ge(bias_parts, 1)
            sp.dma_start(bias_rows.rearrange("c e n -> e c n"), bias_p[0:NE]).then_inc(bias_saved, 16)

            def step(i, r, tail):
                if not (tail and r > 0):
                    load(i + (r + 3) // 4, (r + 3) % 4)
                if not (tail and r == 3):
                    put_max(i + (r + 1) // 4, (r + 1) % 4)

            unit_loop(sp, step)

            sp.wait_ge(exp_done, NS * (UNITS + 1) + 3)
            sp.wait_ge(pv_done, KB * UNITS + KB)
            w3v = w3_sb.rearrange("p (e k n) -> p e k n", e=NE, k=HC)
            for e in range(NE):
                sp.dma_start(w3v[:, e, :, :], W3[e].rearrange("(k p) n -> p k n", p=P)
                             ).then_inc(w3_in, 16)
                if e >= NE - late_experts:
                    sp.dma_start(w1v[:, e], W1[e].rearrange("(k p) n -> p k n", p=P)).then_inc(w3_in, 16)
            sp.wait_ge(bias_saved, 16)
            sp.dma_start(b3_sb, bias_rows.rearrange("c e n -> c (e n)")).then_inc(b3_in, 16)

            for b in range(B):
                sp.wait_ge(proj_read, KB * (b + 1))
                sp.dma_start(sums[b * T:(b + 1) * T].rearrange("(k p) d -> p k d", p=P),
                             x_all[:, b * KB:(b + 1) * KB, :]).then_inc(sums_in, 16)
            sp.dma_start(sums[N:], x_all[:, 0, :]).then_inc(sums_in, 16)
            sp.wait_ge(added, 16 * NT)
            sp.dma_start(out.rearrange("b (p t) d -> (b p) (t d)", p=P // B),
                         sums[0:N].rearrange("(p t) d -> p (t d)", p=P)).then_inc(out_saved, 16)
            sp.wait_ge(out_saved, 16)

        @block.gpsimd
        def _(pool):
            own = Steps(pool, consts)
            own.done(pool.memset(ident[:, :], 0.0))
            own.done(pool.memset(identb[:, :], 0.0))
            own.done(pool.memset(causal[:, :], 0.0))
            own.done(pool.memset(below[:, :], 1.0))
            own.done(pool.memset(onesb[:, :], 1.0))
            own.done(pool.memset(minus1[0:3, :], -1.0))
            own.done(pool.memset(no_slot[:, :, 1], 0.0))
            own.wait()
            for m in (ident, identb):
                own.done(pool.affine_select(out=m[:, :], in_=m[:, :], compare_op=ALU.not_equal, fill=1.0,
                                            base=0, pattern=[[-1, P]], channel_multiplier=1))
            own.done(pool.affine_select(out=causal[:, :], in_=causal[:, :], compare_op=ALU.is_ge, fill=NEG,
                                        base=0, pattern=[[-1, P]], channel_multiplier=1))
            own.done(pool.affine_select(out=below[:, :], in_=below[:, :], compare_op=ALU.is_gt, fill=0.0,
                                        base=0, pattern=[[1, P]], channel_multiplier=-1))
            own.done(pool.iota(rev8, pattern=[[-1, NE]], base=NE, channel_multiplier=0,
                               allow_small_or_imprecise_dtypes=True))
            own.done(pool.iota(thr, pattern=[[P, TT]], base=0, channel_multiplier=0,
                               allow_small_or_imprecise_dtypes=True))
            own.done(pool.iota(tile_no, pattern=[[1, NT + 1]], base=0, channel_multiplier=0,
                               allow_small_or_imprecise_dtypes=True))
            for c in range(2):
                own.done(pool.iota(pairs[:, c * TT:(c + 1) * TT, 0], pattern=[[P, TT]], base=0,
                                   channel_multiplier=1, allow_small_or_imprecise_dtypes=True))
            own.done(pool.iota(no_slot[:, :, 0], pattern=[[0, NT + 1]], base=N, channel_multiplier=1,
                               allow_small_or_imprecise_dtypes=True))
            assert own.n == CONSTS
            pool.memset(q_ring[:, :, :, :], 0.0).then_inc(rings_set, 1)
            pool.memset(k_ring[:, :, :, :], 0.0).then_inc(rings_set, 1)
            pool.memset(vbuf[:, v_words:], 0.0).then_inc(rings_set, 1)
            pool.memset(v_all[:, :, :, :, VD:VW], 1.0).then_inc(rings_set, 1)
            pool.wait_ge(consts, CONSTS)
            pool.wait_ge(rings_set, 2)
            for r in range(4):
                pool.dma_start(k_ring[MAX_AT:P, r, :, :], minus1[0:3, :].rearrange("p (j n) -> p j n", j=2)
                               ).then_inc(minus_in, 16)
            pool.dma_start(slot_rows.rearrange("(p j) c -> p j c", p=P), no_slot).then_inc(slot_zero, 16)
            pool.wait_ge(w_in, W_IN)

            bs = Steps(pool, bias_step)
            nb = slice(0, NE)
            n = 0
            for b in range(B):
                for f in range(4):
                    pool.wait_ge(part1, n + 1)
                    pool.tensor_tensor(parts[:, n % 4, 2, :], rest[:, n % 2, :], parts[:, n % 4, 1, :],
                                       ALU.subtract).then_inc(part2, 1)
                    n += 1
                if b == 0:
                    bs.then_wait(pool.tensor_copy(bias_p[nb, 0, :], bias_in[nb, :]))
                if b == 1:
                    bs.then_wait(pool.tensor_tensor(bias_r[nb, :], bias_in[nb, :], bias_p[nb, 0, :],
                                                    ALU.subtract))
                if b == 2:
                    bs.then_wait(pool.tensor_copy(bias_p[nb, 1, :], bias_r[nb, :]))
            pool.tensor_tensor(bias_p[nb, 2, :], bias_r[nb, :], bias_p[nb, 1, :], ALU.subtract
                               ).then_inc(bias_parts, 1)

            pool.wait_ge(v_copied, TT)
            pool.wait_ge(rings_set, 4)
            pool.tensor_copy(v_unit[:, 0, :, :, 0:VW], v_all[:, 0]).then_inc(v_ready, 1)
            pool.wait_ge(slots_ready, 1)
            pool.wait_ge(slot_zero, 16)
            pool.wait_ge(rt, RT_STEPS)
            pr = Steps(pool, pool_step)

            def scatter_slots(i, r):
                pr.done(pool.tensor_copy(at_now[:, r, :], column(slot_at[:, :].unsqueeze(2), 4 * i + r)))
                pr.done(pool.tensor_copy(pair_now[:, r, :], column(pairs, 4 * i + r)))
                pr.wait()
                pool.sem_inc(pool_on, 1)
                pool.indirect_dma_start(out=slot_rows, out_offset=bass.IndirectOffsetOnAxis(
                    ap=at_now[:, r, :], axis=0), in_=pair_now[:, r, :], in_offset=None
                ).then_inc(scattered[r], 16)

            def difference(i, r):
                d = column(d_all, i + r // 2)[:, :, 1 - r // 2, :]
                pool.wait_ge(s_read, NS * (4 * i + r + 2) + O_AT + 1 + 3)
                pool.sem_inc(pool_on, 1)
                pool.tensor_tensor(d, a1[:, :, :].rearrange("p (t h) e -> p t (h e)", h=4),
                                   a2[:, :, :].rearrange("p (t h) e -> p t (h e)", h=4), ALU.add
                                   ).then_inc(diff_done, 1)
                pool.wait_ge(diff_done, 2 * i + r // 2 + 1)
                pool.sem_inc(pool_on, 1)
                pr.then_wait(pool.tensor_tensor(squares[:, :, :], d, d, ALU.mult))
                sq = squares[:, :, :].rearrange("p t (h e) -> p t h e", h=4)
                for n in (8, 4, 2):
                    pr.then_wait(pool.tensor_tensor(sq[:, :, :, 0:n], sq[:, :, :, 0:n], sq[:, :, :, n:2 * n],
                                                    ALU.add))
                pool.sem_inc(pool_on, 1)
                pool.tensor_tensor(column(ssq, i + r // 2)[:, :, 1 - r // 2, :].unsqueeze(3), sq[:, :, :, 0:1],
                                   sq[:, :, :, 1:2], ALU.add).then_inc(ssq_done, 1)

            STEPS_OF_4 = 4 * 2 + 2 * 4

            def step(i, r, tail):
                if r == 0:
                    pr.before, pr.n = STEPS_OF_4 * i, 0
                for kb in range(KB):
                    if kb == r % 2:
                        scatter_slots(i, r)
                    pool.wait_ge(exp_done, NS * (4 * i + r + 1) + b_place(B_LAST[kb]) + 1 + 3)
                    pool.sem_inc(pool_on, 1)
                    diag = pt[kb][:, :, 0:P]
                    pool.affine_select(out=diag, in_=diag, compare_op=ALU.is_ge, fill=0.0, base=0,
                                       pattern=[[0, 4], [1, P]], channel_multiplier=-1).then_inc(masked, 1)
                if r % 2 == 0:
                    difference(i, r)
                else:
                    if not (tail and r == 3):
                        pool.wait_ge(pv_done, KB * (4 * i + r))
                        g = 2 * i + (r + 1) // 2
                        pool.tensor_copy(v_unit[:, (r + 1) // 2 % 2, :, :, 0:VW], column(v_all, g)
                                         ).then_inc(v_ready, 1)
                pool.wait_ge(scattered[r], 16 * (i + 1))
                assert r < 3 or pr.n == STEPS_OF_4

            unit_loop(pool, step)

            for b in range(B):
                pool.wait_ge(norms_ready, b + 1)
                scale_pair(pool, b, 1).then_inc(dn_ready[1], 1)
                if b == 0:
                    difference(UNITS // 4, 0)

            pool.dma_start(slot_sb[:, :, :], slot_rows.rearrange("(p j) c -> p j c", p=P)).then_inc(slots_in, 16)
            pool.wait_ge(slots_in, 16)

            ix = Steps(pool, idx_ready)
            ix.done(pool.tensor_copy(token_i[:, :], slot_sb[:, :, 0]))

            def gather(i, q):
                pool.wait_ge(xT_ps, 2 * i + q + 1)
                ix.done(pool.tensor_copy(idx[:, q, :], column(token_i[:, :].unsqueeze(2), 2 * i + q)))
                ix.wait()
                pool.sem_inc(pool_on, 1)
                pool.indirect_dma_start(out=xg[:, q, :], out_offset=None, in_=xn_rows,
                                        in_offset=bass.IndirectOffsetOnAxis(ap=idx[:, q, :], axis=0)
                                        ).then_inc(gathered[q], 16)

            def add_rows(i, q):
                ix.done(pool.tensor_copy(idx[:, 2, :], column(token_i[:, :].unsqueeze(2), 2 * i + q)))
                ix.wait()
                pool.wait_ge(y_ready, 2 * i + q + 1 + 2)
                pool.sem_inc(pool_on, 1)
                pool.indirect_dma_start(out=sums, out_offset=bass.IndirectOffsetOnAxis(
                    ap=idx[:, 2, :], axis=0), in_=ybuf[:, q, :], in_offset=None,
                    compute_op=ALU.add).then_inc(added, 16)
                pool.wait_ge(added, 16 * (2 * i + q) + 16)
                pool.sem_inc(rows_free, 1)

            ix.wait()
            for i in range(2):
                gather(i, 0)
                gather(i, 1)
            pool.wait_ge(sums_in, 16 * (B + 1))
            before = ix.n
            with pool.Fori(0, NT // 2 - 2) as i:
                ix.before, ix.n = before + 4 * i, 0
                for q in range(2):
                    gather(i + 2, q)
                for q in range(2):
                    add_rows(i, q)
            ix.before, ix.n = before + 4 * (NT // 2 - 2), 0
            gather(NT // 2, 0)
            for j in range(NT - 5, NT):
                add_rows(j // 2, j % 2)

        @block.scalar
        def _(act):
            act.dma_start(bgb, bg.rearrange("(o n) -> o n", o=1).broadcast_to([P, NE])).then_inc(w_in, 16)
            for a, v in enumerate((lq1, lk1, lq2, lk2)):
                act.dma_start(lam_in[:, a, :], v.rearrange("(o n) -> o n", o=1).broadcast_to([P, HD])
                              ).then_inc(w_in, 16)
            act.dma_start(bias_in[0:NE, :], b3).then_inc(w_in, 16)
            for l, v in enumerate((b1, b2)):
                act.dma_start(b12[l * NE * HC:(l + 1) * NE * HC, :], v.rearrange("e (c p) -> (e c) p", p=P)
                              ).then_inc(w_in, 16)
            act.dma_start(wproj_sb[:, :, :], Wproj.rearrange("(k p) n -> p k n", p=P)).then_inc(w_in, 16)

            n = 0
            nv = 0

            def deviations(b):
                act.wait_ge(ve_ready, b + 1)
                act.activation(sd[:, b * KB:(b + 1) * KB], ve[:, b * KB:(b + 1) * KB], ACT.Sqrt
                               ).then_inc(sd_ready, 1)

            def copy_xnT(b):
                act.wait_ge(xnT_ps, b + 1)
                if b >= 2:
                    act.wait_ge(vg_ps, KB * (b - 1))
                for k in range(KC):
                    act.activation(xnT[:, b % 2, k, :], bank[k][:, :], ACT.Copy).then_inc(xnT_ready, 1)

            deviations(0)
            deviations(1)
            copy_xnT(0)
            for b in range(B):
                for f in range(4):
                    act.wait_ge(qk_ps, n + 1)
                    if n >= 4:
                        act.wait_ge(stacked[n % 4], 16 * 3 * (n // 4))
                    act.activation(parts[:, n % 4, 0, :], bank[2 + n % 2][:, :], ACT.Copy).then_inc(part0, 1)
                    n += 1
                if b + 1 < B:
                    copy_xnT(b + 1)
                for k in range(KB):
                    act.wait_ge(vg_ps, nv + 1)
                    act.wait_ge(rings_set, 4)
                    act.activation(v_all[:, b * HG:(b + 1) * HG, k, :, 0:VD],
                                   bank[4 + nv % 3][:, 0:D].rearrange("p (g h e) -> p g h e", g=HG, h=4),
                                   ACT.Copy).then_inc(v_copied, 1)
                    nv += 1
                    if b + 2 < B and k == 0:
                        deviations(b + 2)
            act.sem_inc(exp_done, 3)
            act.wait_ge(st_ps, NS)
            act.activation(mT[:, 0, :], B_BANKS[M_AT % 3][0:12, 0:T // 2].bitcast(BF16), ACT.Copy
                           ).then_inc(exp_done, NS)
            act.wait_ge(lam_ready, 1)
            act.activation(lam_e, lam_d, ACT.Exp).then_inc(lam_exp, 1)
            act.wait_ge(ex9_in, 1)
            act.activation(ex9, ex9, ACT.Exp).then_inc(ex9_out, 1)


            def copy_mT(i, r):
                act.wait_ge(st_ps, NS * (4 * i + r) + M_AT + 1)
                act.activation(mT[:, r % 2, :], B_BANKS[M_AT % 3][0:12, 0:T // 2].bitcast(BF16), ACT.Copy
                               ).then_inc(exp_done, 1)

            def copy_outT(i, r):
                act.wait_ge(pv_done, KB * (4 * i + r) + KB)
                act.activation(outT[:, (r + 1) % 2, :], V_BANKS[(r + 1) % 2][:, :], ACT.Copy).then_inc(outT_ready, 1)

            assert UNITS // 4 == NE == (NE - late_experts) * KC and HC % 2 == 0

            def load_weights(i, r):
                if r == 0:
                    act.wait_ge(rt, RT_STEPS)
                    act.wait_ge(slots_ready, 1)
                    act.wait_ge(xn_saved, 16 * 2)
                    act.wait_ge(bias_saved, 16)
                    act.wait_ge(slot_zero, 16)
                    act.wait_ge(minus_in, 16 * 4)
                    for k in range(4):
                        act.wait_ge(stacked[k], 16 * 3 * B)
                if r < 2:
                    half = slice(r * HC // 2, (r + 1) * HC // 2)
                    act.dma_start(column(w2v, i)[:, half], row(W2.rearrange("e (k p) n -> e p k n", p=P), i)[:, half]
                                  ).then_inc(w12_in, 16)
                elif r == 2:
                    act.dma_start(column(w1_sb.rearrange("p (c n) -> p c n", n=H), i),
                                  row(W1.rearrange("e (k p) n -> (e k) p n", p=P), i)).then_inc(w12_in, 16)

            def step(i, r, tail):
                last = tail and r == 3
                for g, (kb, h0, heads, w) in enumerate(B_GROUPS):
                    n = b_place(g)
                    if n == M_AT + 1 and not last:
                        copy_mT(i + (r + 1) // 4, (r + 1) % 4)
                    if g == OUT_AT:
                        load_weights(i, r)
                        copy_outT(i, r)
                    act.wait_ge(st_ps, NS * (4 * i + r + 1) + n + 1)
                    if g == 0 or B_GROUPS[g - 1][0] != kb:
                        act.wait_ge(pv_done, KB * (4 * i + r) + kb + 1)
                    src = B_BANKS[n % 3][:, 0:w * heads].rearrange("p (h n) -> p h n", h=heads)
                    act.activation(pt[kb][:, h0:h0 + heads, :], src, ACT.Exp, scale=SCALE
                                   ).then_inc(exp_done, 2 if last and n == M_AT - 1 else 1)

            act.sem_inc(outT_ready, 1)
            unit_loop(act, step)
            act.wait_ge(ssq_ready, 1)
            act.activation(rms[:, 0:B - 1, :], ssq_b[:, 0:B - 1], ACT.Sqrt).then_inc(rms_ready, 1)
            copy_outT(UNITS // 4, 0)
            for b in range(B):
                act.wait_ge(dT_ps, b + 1)
                if b >= 2:
                    act.wait_ge(proj_ps, KB * (b - 1))
                for k in range(KC):
                    act.activation(dT[b % 2][:, k, :], bank[4 * ((b + 1) % 2) + k][:, :], ACT.Copy
                                   ).then_inc(dT_ready, 1)
                if b == 0:
                    act.wait_ge(ssq_ready, 2)
                    act.activation(rms[:, B - 1, :], ssq_b[:, B - 1], ACT.Sqrt).then_inc(rms_ready, 1)

            act.wait_ge(slots_in, 16)
            act.sem_inc(rows_free, 2)
            act.wait_ge(b12T_ps, 1)
            act.activation(b12T[:, :], bank[7][:, 0:2 * NE * HC], ACT.Copy).then_inc(b12T_ready, 1)
            act.wait_ge(b12T_ready, 1)
            act.sem_inc(y_ready, 2)

            def gelu(layer, i, q):
                e = expert_of(act, i, q)
                act.wait_ge(l_ps[layer], 2 * i + q + 1)
                for c in range(HC):
                    ins = act.activation(hT[layer][:, q, c, :], bank[2 * layer + q][:, c * P:(c + 1) * P], ACT.Gelu,
                                         bias=b12T[:, bass.ds((layer * NE + e) * HC + c, 1)])
                ins.then_inc(h_ready[layer], 1)

            def rows_out(i, q):
                act.wait_ge(y_ps, 2 * i + q + 1)
                act.wait_ge(rows_free, 2 * i + q + 1)
                act.activation(ybuf[:, q, :], bank[6 + q][:, 0:D], ACT.Copy,
                               scale=column(slot_sb, 2 * i + q)[:, 1:2]).then_inc(y_ready, 1)

            gelu(0, 0, 0)
            gelu(0, 0, 1)

            def experts(i, pair, ahead):
                for q in pair:
                    gelu(1, i, q)
                for q in pair:
                    if q in ahead:
                        gelu(0, i + 1, q)
                    rows_out(i, q)

            tile_loop(act, experts)

        @block.vector
        def _(dve):
            st = Steps(dve, ln)
            n = 0
            nv = 0

            def norm_stats(t):
                if t % KB == 0:
                    dve.wait_ge(x_in[t // KB], 16)
                st.done(dve.bn_stats(stats[:, t, :], x_all[:, t, :]))

            def norm_variances(b):
                t0, t1 = b * KB, (b + 1) * KB
                st.wait()
                for t in range(t0, t1):
                    st.done(dve.bn_aggr(mv[:, t, :], stats[:, t, :]))
                st.wait()
                dve.tensor_scalar(ve[:, t0:t1], mv[:, t0:t1, 1], EPS, None, ALU.add).then_inc(ve_ready, 1)

            def norm_scales(b):
                t0, t1 = b * KB, (b + 1) * KB
                dve.wait_ge(sd_ready, b + 1)
                st.then_wait(dve.reciprocal(rstd[:, t0:t1], sd[:, t0:t1]))
                st.then_wait(dve.tensor_tensor(nwt[:, t0:t1], rstd[:, t0:t1], rstd[:, t0:t1], ALU.mult))
                st.then_wait(dve.tensor_tensor(nwt[:, t0:t1], nwt[:, t0:t1], ve[:, t0:t1], ALU.mult))
                st.then_wait(dve.tensor_scalar(nwt[:, t0:t1], nwt[:, t0:t1], -0.5, 1.5, ALU.mult, ALU.add))
                st.then_wait(dve.tensor_tensor(rstd[:, t0:t1], rstd[:, t0:t1], nwt[:, t0:t1], ALU.mult))

            def norm_rows(t):
                dve.tensor_scalar(xn_all[:, t, :], x_all[:, t, :], mv[:, t, 0:1], rstd[:, t:t + 1],
                                  ALU.subtract, ALU.mult).then_inc(xn_ready, 1)

            def norm(b):
                for t in range(b * KB, (b + 1) * KB):
                    norm_stats(t)
                norm_variances(b)
                norm_scales(b)
                for t in range(b * KB, (b + 1) * KB):
                    norm_rows(t)

            def maxima(i, r, g, first=False):
                t, h0, heads, w = A_GROUPS[g]
                n = a_place(g)
                dve.wait_ge(s_ps, NS * (4 * i + r) + n + 1)
                src = A_BANKS[n % 3][:, 0:w * heads].rearrange("p (h n) -> p h n", h=heads)
                dve.tensor_reduce(mx[:, r % 2, h0:h0 + heads, t], src, X, ALU.max
                                  ).then_inc(s_read, 2 if first and n == O_AT - 1 else 1)

            def max_part(i, r, k):
                m, rr = mx[:, r % 2], mrest[:, r % 2]
                mp = mparts[:, r % 2].rearrange("p t c h -> p h t c")
                if k == 0:
                    dve.wait_ge(s_read, NS * (4 * i + r + 1) + 3)
                    dve.tensor_copy(mp[:, :, :, 0], m).then_inc(mx_step, 1)
                else:
                    dve.wait_ge(mx_step, 3 * (4 * i + r) + k)
                if k == 1:
                    dve.tensor_tensor(rr, m, mp[:, :, :, 0], ALU.subtract).then_inc(mx_step, 1)
                if k == 2:
                    dve.tensor_copy(mp[:, :, :, 1], rr).then_inc(mx_step, 1)
                if k == 3:
                    dve.tensor_tensor(mp[:, :, :, 2], rr, mp[:, :, :, 1], ALU.subtract).then_inc(mp_ready, 1)

            dve.sem_inc(s_read, 3)
            norm(0)
            norm(1)
            dve.wait_ge(w_in, W_IN)
            st.then_wait(dve.tensor_tensor(lam_pr, lam_in[:, 0:4:2, :], lam_in[:, 1:4:2, :], ALU.mult))
            dve.tensor_reduce(lam_d, lam_pr, X, ALU.add).then_inc(lam_ready, 1)
            for b in range(B):
                for f in range(4):
                    dve.wait_ge(part0, n + 1)
                    if n >= 2:
                        dve.wait_ge(part2, n - 1)
                    dve.tensor_tensor(rest[:, n % 2, :], bank[2 + n % 2][:, :], parts[:, n % 4, 0, :],
                                      ALU.subtract).then_inc(rest_ready, 1)
                    if n >= 4:
                        dve.wait_ge(stacked[n % 4], 16 * 3 * (n // 4))
                    dve.wait_ge(rest_ready, n + 1)
                    dve.tensor_copy(parts[:, n % 4, 1, :], rest[:, n % 2, :]).then_inc(part1, 1)
                    n += 1
                    if b == B - 1:
                        for g in EARLY[f]:
                            maxima(0, 0, g, first=True)
                    if b + 2 < B:
                        norm_stats((b + 2) * KB + f)
                if b + 2 < B:
                    norm_variances(b + 2)
                if b == B - 1:
                    for k in range(4):
                        max_part(0, 0, k)
                for k in range(KB):
                    dve.wait_ge(vg_ps, nv + 1)
                    dve.wait_ge(v_copied, nv + 1)
                    dve.tensor_tensor(logits[:, nv, :], bank[4 + nv % 3][:, D:D + NE], bgb, ALU.add
                                      ).then_inc(lg_ready, 1)
                    nv += 1
                    if b == B - 1:
                        for g in EARLY[k]:
                            maxima(0, 1, g, first=True)
                    if b + 2 < B and k == 1:
                        norm_scales(b + 2)
                    if b + 2 < B and k >= 1:
                        norm_rows((b + 2) * KB + k - 1)
                if b + 2 < B:
                    norm_rows((b + 3) * KB - 1)

            s = Steps(dve, rt)
            do = s.then_wait

            def over_e(v):
                return v.unsqueeze(2).to_broadcast([P, TT, NE])

            dve.wait_ge(lg_ready, TT)
            dve.wait_ge(consts, CONSTS)
            rev = rev8.unsqueeze(1).to_broadcast([P, TT, NE])
            for lg, m, w, oh in ((logits, m1, wm, oh1), (lg2, m2, wm2, oh2)):
                if lg is lg2:
                    do(dve.scalar_tensor_tensor(out=lg2, in0=oh1, scalar=NEG, in1=logits,
                                                op0=ALU.mult, op1=ALU.add))
                do(dve.tensor_reduce(m, lg, X, ALU.max))
                do(dve.tensor_tensor(eq, lg, over_e(m), ALU.is_equal))
                do(dve.tensor_tensor(eq, eq, rev, ALU.mult))
                do(dve.tensor_reduce(w, eq, X, ALU.max))
                do(dve.tensor_tensor(oh, eq, over_e(w), ALU.is_equal))
            dve.tensor_tensor(oh12, oh1, oh2, ALU.add).then_inc(oh_ready, 1)
            do(dve.tensor_tensor(ex9[:, :, 0:NE], logits, over_e(m1), ALU.subtract))
            dve.tensor_tensor(ex9[:, :, NE:9], m2.unsqueeze(2), m1.unsqueeze(2), ALU.subtract
                              ).then_inc(ex9_in, 1)
            dve.wait_ge(lam_exp, 1)
            do(dve.tensor_tensor(neglam[:, :], lam_e[:, 1:2], lam_e[:, 0:1], ALU.subtract))
            do(dve.tensor_scalar(neglam[:, :], neglam[:, :], -LAMBDA_INIT, None, ALU.add))
            dve.wait_ge(rank_ps, 2)
            do(dve.tensor_copy(cnt, bank[6][:, 0:NE]))
            do(dve.tensor_tensor(full, cnt.unsqueeze(2).to_broadcast([P, NE, TT]),
                                 thr.unsqueeze(1).to_broadcast([P, NE, TT]), ALU.is_gt))
            do(dve.tensor_reduce(ctile, full, X, ALU.add))
            do(dve.memset(base[:, 0:1], 0.0))
            for e in range(1, NE):
                do(dve.tensor_tensor(base[:, e:e + 1], base[:, e - 1:e], ctile[:, e - 1:e], ALU.add))
            do(dve.tensor_scalar(base128, base, float(P), None, ALU.mult))
            do(dve.tensor_tensor(pos, bank[4][:, 0:TT * NE].rearrange("p (t e) -> p t e", e=NE),
                                 base128.unsqueeze(1).to_broadcast([P, TT, NE]), ALU.add))
            for c, oh in enumerate((oh1, oh2)):
                do(dve.tensor_tensor(eq, pos, oh, ALU.mult))
                do(dve.tensor_reduce(slot_f[:, c * TT:(c + 1) * TT], eq, X, ALU.add))
            do(dve.tensor_copy(slots_i, slot_f))
            do(dve.tensor_scalar(slot_lo, slots_i, P - 1, None, ALU.bitwise_and))
            do(dve.tensor_scalar(slot_hi, slots_i, 7, None, ALU.logical_shift_right))
            do(dve.tensor_scalar(slot_lo, slot_lo, float(NT + 1), None, ALU.mult))
            dve.tensor_tensor(slot_at[:, :], slot_lo, slot_hi, ALU.add).then_inc(slots_ready, 1)
            do(dve.tensor_tensor(past, tile_no.unsqueeze(2).to_broadcast([P, NT + 1, NE - 1]),
                                 base[:, 1:NE].unsqueeze(1).to_broadcast([P, NT + 1, NE - 1]), ALU.is_ge))
            do(dve.tensor_reduce(texp_f, past, X, ALU.add))
            do(dve.tensor_copy(texp[:, :], texp_f))
            dve.wait_ge(ex9_out, 1)
            do(dve.tensor_reduce(esum, ex9[:, :, 0:NE], X, ALU.add))
            do(dve.reciprocal(wts[:, 0, :], esum))
            do(dve.tensor_tensor(wts[:, 1, :], ex9[:, :, NE], wts[:, 0, :], ALU.mult))
            do(dve.memset(V_BANKS[1][:, :], 1.0))
            do(dve.memset(a1[:, :, :], 0.0))
            assert s.n == RT_STEPS, s.n

            rows_of_bank = A_BANKS[O_AT % 3][:, :].rearrange("p (g e) -> p g e", e=32)

            def normalize(i, r, alone=False):
                dve.wait_ge(s_ps, NS * (4 * i + r + 2) + (NS if alone else O_AT + 1))
                dve.reciprocal(rsum[:, r % 2, :], rows_of_bank[:, :, VD]).then_inc(at_step, 1)
                rs = rsum[:, r % 2, :].unsqueeze(2).to_broadcast([P, 4 * KB, VD])
                o = rows_of_bank[:, :, 0:VD]
                dve.wait_ge(at_step, 4 * i + r + 1)
                if r % 2 == 0:
                    dve.scalar_tensor_tensor(out=a2[:, :, :], in0=o, scalar=neglam[:, 0:1], in1=rs,
                                             op0=ALU.mult, op1=ALU.mult).then_inc(s_read, NS if alone else 1)
                else:
                    dve.wait_ge(diff_done, 2 * i + r // 2 + 1)
                    dve.tensor_tensor(a1[:, :, :], o, rs, ALU.mult).then_inc(s_read, NS if alone else 1)

            def step(i, r, tail):
                ahead = not (tail and r >= 2)
                i1, r1 = i + (r + 1) // 4, (r + 1) % 4
                i2, r2 = i + (r + 2) // 4, (r + 2) % 4
                if not (tail and r == 3):
                    dve.wait_ge(st_ps, NS * (4 * i + r) + M_AT + 1)
                for g in range(NG):
                    if g < 2 and not (tail and r == 3):
                        max_part(i1, r1, 2 * g)
                        max_part(i1, r1, 2 * g + 1)
                    if a_place(g) == O_AT + 1:
                        normalize(i, r, alone=not ahead)
                    if ahead:
                        maxima(i2, r2, g)

            unit_loop(dve, step)
            e = Steps(dve, ep)
            c = 1.0 - LAMBDA_INIT

            def mean_squares(b0, b1):
                dve.wait_ge(ssq_done, HG * b1 + 1)
                dve.tensor_scalar(ssq_b[:, b0:b1], ssq_b[:, b0:b1], 1.0 / VD, EPS, ALU.mult, ALU.add
                                  ).then_inc(ssq_ready, 1)

            def norms(b):
                dve.wait_ge(rms_ready, 1 if b < B - 1 else 2)
                e.then_wait(dve.reciprocal(rinv[:, b, :], rms[:, b, :]))
                e.then_wait(dve.tensor_tensor(rms[:, b, :], rinv[:, b, :], rinv[:, b, :], ALU.mult))
                e.then_wait(dve.tensor_tensor(rms[:, b, :], rms[:, b, :], ssq_b[:, b, :], ALU.mult))
                e.then_wait(dve.tensor_scalar(rms[:, b, :], rms[:, b, :], -0.5 * c, 1.5 * c, ALU.mult, ALU.add))
                dve.tensor_tensor(rinv[:, b, :], rinv[:, b, :], rms[:, b, :], ALU.mult).then_inc(norms_ready, 1)
                dve.wait_ge(norms_ready, b + 1)
                scale_pair(dve, b, 0).then_inc(dn_ready[0], 1)

            mean_squares(0, B - 1)
            norms(0)
            normalize(UNITS // 4, 0, alone=True)
            for b in range(1, B - 1):
                norms(b)
            mean_squares(B - 1, B)
            norms(B - 1)
            for tt in range(TT):
                dve.wait_ge(proj_ps, tt + 1)
                dve.tensor_tensor(x_all[:, tt, :], x_all[:, tt, :], bank[2 + tt % 2][:, 0:D], ALU.add
                                  ).then_inc(proj_read, 1)

            def copy_xT(i, q):
                dve.wait_ge(xT_ps, 2 * i + q + 1 + 2)
                dve.tensor_copy(xT[:, q, :, :], bank[4 + q][:, 0:KC * P].rearrange(
                    "p (k n) -> p k n", k=KC)).then_inc(xT_ready, 1)

            def copy_w(l, q, e):
                w, now, n = ((w1_sb, w1_now[q], KC * H), (w2_sb, w2_now[:, q], HC * H))[l]
                dve.tensor_copy(now, w[:, bass.ds(e * n, n)]).then_inc(w_ready[l], 1)

            def experts(i, pair, ahead):
                e = [expert_of(dve, i + 1, q) for q in ahead]
                for q in ahead:
                    dve.wait_ge(l_ps[0], 2 * i + q + 1)
                    copy_xT(i + 1, q)
                    copy_w(0, q, e[q])
                for q in ahead:
                    dve.wait_ge(l_ps[1], 2 * i + q + 1)
                    copy_w(1, q, e[q])

            dve.wait_ge(w12_in, 16 * 3 * (UNITS // 4))
            dve.wait_ge(w3_in, 16 * (NE + late_experts))
            e = [expert_of(dve, 0, q) for q in range(2)]
            for q in range(2):
                copy_xT(0, q)
                copy_w(0, q, e[q])
            dve.wait_ge(sums_in, 16 * (B + 1))
            for q in range(2):
                copy_w(1, q, e[q])
            tile_loop(dve, experts)

        @block.tensor
        def _(pe):
            pe.wait_ge(w_in, W_IN)
            pe.wait_ge(consts, CONSTS)
            pe.sem_inc(pv_done, KB)
            pe.sem_inc(xT_ps, 2)

            def transposes(b):
                pe.wait_ge(xn_ready, KB * (b + 1))
                if b > 0:
                    pe.wait_ge(xnT_ready, KC * b)
                for k in range(KC):
                    for t in range(KB):
                        mm = pe.transpose(bank[k][:, t * P:(t + 1) * P],
                                          xn_all[:, b * KB + t, k * P:(k + 1) * P], ident[:, :])
                mm.then_inc(xnT_ps, 1)

            def scores(i, r, g, first=False):
                t, h0, heads, w = A_GROUPS[g]
                if g == 0:
                    pe.wait_ge(unit_in[r], 16 * 4 * (i + 1))
                n = a_place(g)
                pe.wait_ge(s_read, NS * (4 * i + r) + n + 1)
                for c in range(heads):
                    o = A_BANKS[n % 3][:, c * w:(c + 1) * w]
                    pe.matmul(o, q_ring[0:MAX_AT, r, h0 + c, t * P:(t + 1) * P],
                              k_ring[0:MAX_AT, r, (h0 + c) % 2, 0:w], start=True, stop=False)
                    mm = pe.matmul(o[:, t * P:(t + 1) * P], identb[:, :], causal[:, :], start=False, stop=True)
                mm.then_inc(s_ps, 2 if first and n == O_AT - 1 else 1)

            n = 0
            nv = 0
            transposes(0)
            for b in range(B):
                pe.wait_ge(xnT_ready, KC * (b + 1))
                for f in range(4):
                    if n >= 2:
                        pe.wait_ge(rest_ready, n - 1)
                    for k in range(KC):
                        mm = pe.matmul(bank[2 + n % 2][:, :], wqk[:, k, f * P:(f + 1) * P], xnT[:, b % 2, k, :],
                                       start=(k == 0), stop=(k == KC - 1))
                    mm.then_inc(qk_ps, 1)
                    n += 1
                    if b == B - 1:
                        for g in EARLY[f]:
                            scores(0, 0, g, first=True)
                if b + 1 < B:
                    transposes(b + 1)
                for t in range(KB):
                    if nv >= 3:
                        pe.wait_ge(lg_ready, nv - 2)
                    for k in range(KC):
                        mm = pe.matmul(bank[4 + nv % 3][:, 0:D + NE], xnT[:, b % 2, k, t * P:(t + 1) * P],
                                       wvg[:, k, :], start=(k == 0), stop=(k == KC - 1))
                    mm.then_inc(vg_ps, 1)
                    nv += 1
                    if b == B - 1:
                        for g in EARLY[t]:
                            scores(0, 1, g, first=True)

            def scores_T(i, r, g):
                kb, h0, heads, w = B_GROUPS[g]
                if g == 0:
                    pe.wait_ge(max_rows[r], 16 * (i + 1))
                n = b_place(g)
                pe.wait_ge(exp_done, NS * (4 * i + r + 1) + n + 1)
                for c in range(heads):
                    mm = pe.matmul(B_BANKS[n % 3][:, c * w:(c + 1) * w],
                                   k_ring[:, r, (h0 + c) % 2, kb * P:(kb + 1) * P],
                                   q_ring[:, r, h0 + c, kb * P:T], start=True, stop=True)
                last = isinstance(i, int) and 4 * i + r == UNITS - 1
                mm.then_inc(st_ps, 2 if last and n == M_AT - 1 else 1)

            def values(i, r, kb):
                if kb == 0:
                    pe.wait_ge(outT_ready, 4 * i + r + 1)
                    pe.wait_ge(v_ready, 2 * i + r // 2 + 1)
                pe.wait_ge(masked, KB * (4 * i + r) + kb + 1)
                for hh in range(4):
                    mm = pe.matmul(V_BANKS[r % 2][32 * hh:32 * hh + 32, kb * P:T], v_unit[:, r // 2, kb, hh, :],
                                   pt[kb][:, hh, :], start=(kb == 0), stop=(kb == KB - 1),
                                   skip_group_check=True)
                mm.then_inc(pv_done, 1)

            def turn_rows(i, r, alone=False):
                pe.wait_ge(outT_ready, 4 * i + r + 1 + 1)
                pe.wait_ge(s_read, NS * (4 * i + r + 2) + (3 if alone else O_AT + 1))
                for t in range(KB):
                    mm = pe.transpose(A_BANKS[O_AT % 3][:, t * P:(t + 1) * P],
                                      outT[:, (r + 1) % 2, t * P:(t + 1) * P], ident[:, :])
                mm.then_inc(s_ps, NS if alone else 1)

            def turn_max(i, r, alone=False):
                pe.wait_ge(mp_ready, 4 * i + r + 1)
                pe.wait_ge(exp_done, 3 if alone else NS * (4 * i + r) + M_AT + 1)
                for t in range(KB):
                    mm = pe.transpose(B_BANKS[M_AT % 3][0:12, t * P // 2:(t + 1) * P // 2].bitcast(BF16),
                                      mparts[:, r % 2, t, :, :].rearrange("p c h -> p (c h)"), identb[:, :])
                mm.then_inc(st_ps, NS if alone else 1)

            def ranks():
                pe.wait_ge(oh_ready, 1)
                mm = pe.matmul(bank[4][:, 0:TT * NE], below[:, :], oh12.rearrange("p t e -> p (t e)"),
                               start=True, stop=False, skip_group_check=True)
                for t in range(TT - 1):
                    mm = pe.matmul(bank[4][:, (t + 1) * NE:TT * NE].rearrange("p (t e) -> p t e", e=NE), onesb[:, :],
                                   oh12[:, t:t + 1, :].to_broadcast([P, TT - 1 - t, NE]),
                                   start=False, stop=(t == TT - 2), skip_group_check=True)
                mm.then_inc(rank_ps, 1)
                for t in range(TT):
                    mm = pe.matmul(bank[6][:, 0:NE], onesb[:, :], oh12[:, t, :], start=(t == 0), stop=(t == TT - 1))
                mm.then_inc(rank_ps, 1)

            pe.wait_ge(lg_ready, TT)
            turn_max(0, 0, alone=True)
            ranks()

            def step(i, r, tail):
                ahead = not (tail and r >= 2)
                a, b, v = iter(range(NG)), iter(range(B_AHEAD, NG + B_AHEAD)), iter(range(KB))
                for what in ORDER:
                    if what == "A" and ahead:
                        scores(i + (r + 2) // 4, (r + 2) % 4, next(a))
                    if what == "B":
                        g = next(b)
                        if g < NG:
                            scores_T(i, r, g)
                        elif not (tail and r == 3):
                            scores_T(i + (r + 1) // 4, (r + 1) % 4, g - NG)
                    if what == "V":
                        values(i, r, next(v))
                    if what == "o":
                        turn_rows(i, r, alone=not ahead)
                    if what == "m" and not (tail and r == 3):
                        turn_max(i + (r + 1) // 4, (r + 1) % 4)

            for g in range(B_AHEAD):
                scores_T(0, 0, g)
            unit_loop(pe, step)
            turn_rows(UNITS // 4, 0, alone=True)

            def turn_differences(b):
                for k in range(KC):
                    pe.wait_ge(dn_ready[k], b + 1)
                    if b >= 2:
                        pe.wait_ge(dT_ready, KC * (b - 1))
                    for t in range(KB):
                        mm = pe.transpose(bank[4 * ((b + 1) % 2) + k][:, t * P:(t + 1) * P],
                                          d_all[:, 1 + b * HG // 2 + k, t].rearrange("p s n -> p (s n)"),
                                          ident[:, :])
                mm.then_inc(dT_ps, 1)

            turn_differences(0)
            for b in range(B):
                if b + 1 < B:
                    turn_differences(b + 1)
                pe.wait_ge(dT_ready, KC * (b + 1))
                for t in range(KB):
                    tt = b * KB + t
                    if tt >= 2:
                        pe.wait_ge(proj_read, tt - 1)
                    for k in range(KC):
                        mm = pe.matmul(bank[2 + tt % 2][:, 0:D], dT[b % 2][:, k, t * P:(t + 1) * P],
                                       wproj_sb[:, k, :], start=(k == 0), stop=(k == KC - 1))
                    mm.then_inc(proj_ps, 1)

            pe.wait_ge(proj_read, TT)
            pe.wait_ge(w12_in, 16 * 3 * (UNITS // 4))
            pe.wait_ge(w3_in, 16 * (NE + late_experts))
            pe.wait_ge(b3_in, 16)
            pe.transpose(bank[7][:, 0:2 * NE * HC], b12[:, :], ident[0:2 * NE * HC, 0:2 * NE * HC]).then_inc(b12T_ps, 1)

            def turn_x(i, q):
                pe.wait_ge(gathered[q], 16 * (i + 1))
                for k in range(KC):
                    mm = pe.transpose(bank[4 + q][:, k * P:(k + 1) * P], xg[:, q, k * P:(k + 1) * P], ident[:, :])
                mm.then_inc(xT_ps, 1)

            def layer(o, rows, chunks, w):
                for c in range(HC):
                    for k in range(chunks):
                        mm = pe.matmul(o[:, c * P:(c + 1) * P], w[:, k * H + c * P:k * H + (c + 1) * P],
                                       rows[:, k, :], start=(k == 0), stop=(k == chunks - 1))
                return mm

            def layer1(i, q):
                pe.wait_ge(xT_ready, 2 * i + q + 1)
                pe.wait_ge(w_ready[0], 2 * i + q + 1)
                layer(bank[q], xT[:, q], KC, w1_now[q]).then_inc(l_ps[0], 1)

            def layer2(i, q):
                pe.wait_ge(h_ready[0], 2 * i + q + 1)
                pe.wait_ge(w_ready[1], 2 * i + q + 1)
                layer(bank[2 + q], hT[0][:, q], HC, w2_now[:, q]).then_inc(l_ps[1], 1)

            def layer3(i, q):
                e = expert_of(pe, i, q)
                pe.wait_ge(h_ready[1], 2 * i + q + 1)
                pe.wait_ge(y_ready, 2 * i + q + 1)
                y = bank[6 + q][:, 0:D]
                pe.matmul(y, onesb[0:3, :], b3_sb[:, bass.ds(e * D, D)], start=True, stop=False)
                for k in range(HC):
                    mm = pe.matmul(y, hT[1][:, q, k, :], w3_sb[:, bass.ds((e * HC + k) * D, D)],
                                   start=False, stop=(k == HC - 1))
                mm.then_inc(y_ps, 1)

            turn_x(0, 0)
            turn_x(0, 1)
            layer1(0, 0)
            layer1(0, 1)

            def experts(i, pair, ahead):
                for q in pair:
                    if q in ahead:
                        turn_x(i + 1, q)
                    layer2(i, q)
                for q in pair:
                    if q in ahead:
                        layer1(i + 1, q)
                    layer3(i, q)

            tile_loop(pe, experts)


_INS = ['L0_attn_x', 'L0_attn_Wqkv', 'L0_attn_Wproj', 'L0_attn_lambda_q1', 'L0_attn_lambda_k1',
        'L0_attn_lambda_q2', 'L0_attn_lambda_k2', 'L0_ffn_W1', 'L0_ffn_b1', 'L0_ffn_W2', 'L0_ffn_b2',
        'L0_ffn_W3', 'L0_ffn_b3', 'L0_ffn_Wg', 'L0_ffn_bg']


def kernel(**inputs):
    import numpy as _np
    import concourse.bacc as _bacc
    from concourse import mybir as _mybir
    from concourse.bass_utils import run_bass_kernel_spmd as _run

    nc = _bacc.Bacc("TRN2", target_bir_lowering=False, num_devices=1)
    arrays, args = {}, []
    for name in _INS:
        a = _np.ascontiguousarray(inputs[name])
        arrays[f"in_{name}"] = a
        args.append(nc.dram_tensor(f"in_{name}", a.shape, _mybir.dt.from_np(a.dtype), kind="ExternalInput").ap())
    shape = inputs['L0_attn_x'].shape
    args.append(nc.dram_tensor("out_0", shape, _mybir.dt.float32, kind="ExternalOutput").ap())
    build(nc, *args)
    r = _run(nc, [arrays], core_ids=[0])
    return r.results[0]["out_0"]
```
